# Optimizing a Trainium2 kernel written in Bass

```python
import numpy as np
import jax
import jax.numpy as jnp

def _softmax(x, axis=-1):
    return jax.nn.softmax(x, axis=axis)
def _gelu(x):
    return jax.nn.gelu(x, approximate=True)
def _silu(x):
    return jax.nn.silu(x)
def _sigmoid(x):
    return jax.nn.sigmoid(x)
def _layernorm(x, axis=-1, eps=1e-5):
    m = jnp.mean(x, axis=axis, keepdims=True)
    v = jnp.var(x, axis=axis, keepdims=True)
    return (x - m) / jnp.sqrt(v + eps)
def _scatter_add(tgt, idx, src, axis=0):
    return tgt.at[idx].add(src)
def _segment_sum(src, seg, n):
    return jax.ops.segment_sum(src, seg, n)

kernel_name = 'mk_conv_preact_d2_conv_nhwc64_85dc10'

def setup_inputs(seed: int = 0):
    np.random.seed(seed)
    _w = jnp.asarray
    def _rec_inputs():
        import jax
        import jax.numpy as jnp
        _gk = jax.random.key(seed)
        x = -0.000125 + 0.9999 * jax.random.normal(jax.random.fold_in(_gk, 1), (8, 256, 256, 64), jnp.float32)
        return x
    x = _rec_inputs()
    def _L0_conv_setup():
        import jax, jax.numpy as jnp
        import numpy as np
        MODES = 16
        DIMS = 2
        WIDTH = 64
        key = jax.random.key(seed)
        k1, k2, k3, k4 = jax.random.split(key, 4)
        scale = 1.0 / (np.sqrt(2.0) * WIDTH * WIDTH)
        bound = np.sqrt(1.0 / WIDTH)
        x = jax.random.normal(k1, (8, 256, 256, WIDTH), dtype=jnp.float32)
        conv = scale * jax.random.normal(k2, (2, MODES, MODES, WIDTH, WIDTH), dtype=jnp.float32)
        skip_kernel = jax.random.uniform(k3, (WIDTH, WIDTH), minval=-bound, maxval=bound, dtype=jnp.float32)
        skip_bias = jax.random.uniform(k4, (WIDTH,), minval=-bound, maxval=bound, dtype=jnp.float32)
        return {'x': x, 'conv': conv, 'skip_kernel': skip_kernel, 'skip_bias': skip_bias}
    _L0_conv_all = _L0_conv_setup()
    _L0_conv_in = {k: v for k, v in _L0_conv_all.items() if k in ('conv', 'skip_kernel', 'skip_bias', )}
    del _L0_conv_all

    def _L1_conv_setup():
        import jax, jax.numpy as jnp
        import numpy as np

        def _complex_matmul_2d(a, w):
            wr, wi = (w[..., 0], w[..., 1])
            ar, ai = (jnp.real(a), jnp.imag(a))
            out_r = jnp.einsum('bixy,ioxy->boxy', ar, wr) - jnp.einsum('bixy,ioxy->boxy', ai, wi)
            out_i = jnp.einsum('bixy,ioxy->boxy', ai, wr) + jnp.einsum('bixy,ioxy->boxy', ar, wi)
            return out_r + 1j * out_i
        key = jax.random.key(seed)
        ks = jax.random.split(key, 5)
        B, M, N, C, NM = (16, 256, 256, 64, 32)
        x = jax.random.normal(ks[0], (B, M, N, C), dtype=jnp.float32)
        fw_scale = 1.0 / (C * C) ** 0.5 * 0.5
        fw1 = jax.random.normal(ks[1], (C, C, NM, NM, 2), dtype=jnp.float32) * fw_scale
        fw2 = jax.random.normal(ks[2], (C, C, NM, NM, 2), dtype=jnp.float32) * fw_scale
        W = jax.random.normal(ks[3], (C, C), dtype=jnp.float32) * (1.0 / C ** 0.5)
        b = jnp.zeros((C,), dtype=jnp.float32)
        return {'x': x, 'fw1': fw1, 'fw2': fw2, 'W': W, 'b': b}
    _L1_conv_all = _L1_conv_setup()
    _L1_conv_in = {k: v for k, v in _L1_conv_all.items() if k in ('fw1', 'fw2', 'W', 'b', )}
    del _L1_conv_all

    return {
        "x": x,
        "L0_conv_conv": _L0_conv_in["conv"],
        "L0_conv_skip_kernel": _L0_conv_in["skip_kernel"],
        "L0_conv_skip_bias": _L0_conv_in["skip_bias"],
        "L1_conv_fw1": _L1_conv_in["fw1"],
        "L1_conv_fw2": _L1_conv_in["fw2"],
        "L1_conv_W": _L1_conv_in["W"],
        "L1_conv_b": _L1_conv_in["b"],
    }

def reference(x, L0_conv_conv, L0_conv_skip_kernel, L0_conv_skip_bias, L1_conv_fw1, L1_conv_fw2, L1_conv_W, L1_conv_b):
    import jax
    import jax.numpy as jnp
    def _L0_conv_ref(x, conv, skip_kernel, skip_bias):
        import jax, jax.numpy as jnp
        import numpy as np
        MODES = 16
        DIMS = 2
        WIDTH = 64
        spatial = x.shape[-DIMS - 1:-1]
        w = conv[0] + 1j * conv[1]
        x_ft = jnp.fft.rfftn(x, axes=(-3, -2))
        x_ft_trunc = x_ft[..., :MODES, :MODES, :]
        out_trunc = jnp.einsum('bxyi,xyio->bxyo', x_ft_trunc, w)
        out_ft = jnp.zeros(x_ft.shape[:-1] + (WIDTH,), dtype=x_ft.dtype)
        out_ft = out_ft.at[..., :MODES, :MODES, :].set(out_trunc)
        spectral = jnp.fft.irfftn(out_ft, s=spatial, axes=(-3, -2))
        skip = x @ skip_kernel + skip_bias
        return spectral + skip

    def _L1_conv_ref(x, fw1, fw2, W, b):
        import jax, jax.numpy as jnp
        import numpy as np

        def _complex_matmul_2d(a, w):
            wr, wi = (w[..., 0], w[..., 1])
            ar, ai = (jnp.real(a), jnp.imag(a))
            out_r = jnp.einsum('bixy,ioxy->boxy', ar, wr) - jnp.einsum('bixy,ioxy->boxy', ai, wi)
            out_i = jnp.einsum('bixy,ioxy->boxy', ai, wr) + jnp.einsum('bixy,ioxy->boxy', ar, wi)
            return out_r + 1j * out_i
        B, M, N, C = x.shape
        nm = fw1.shape[2]
        O = fw1.shape[1]
        xt = jnp.transpose(x, (0, 3, 1, 2))
        scale_fwd = jnp.sqrt(jnp.asarray(M * N, dtype=jnp.float32))
        x_ft = jnp.fft.rfft2(xt, s=(M, N)) / scale_fwd
        a = x_ft[:, :, :nm, :nm]
        blk1 = _complex_matmul_2d(a, fw1)
        blk2 = _complex_matmul_2d(a, fw2)
        out_ft = jnp.zeros((B, O, N, M // 2 + 1), dtype=x_ft.dtype)
        out_ft = out_ft.at[:, :, :nm, :nm].set(blk1)
        out_ft = out_ft.at[:, :, N - nm:, :nm].set(blk2)
        out = jnp.fft.irfft2(out_ft, s=(N, M))
        scale_bwd = jnp.sqrt(jnp.asarray(N * (M // 2 + 1), dtype=jnp.float32))
        out = out / scale_bwd
        out = jnp.transpose(out, (0, 2, 3, 1))
        res = out @ W + b
        return jax.nn.relu(res + out)

    def _gn(v, G=32, eps=1e-5):
        B_, H_, W_, C_ = v.shape
        g = v.reshape(B_, H_, W_, G, C_ // G)
        m = jnp.mean(g, axis=(1, 2, 4), keepdims=True)
        s = jnp.var(g, axis=(1, 2, 4), keepdims=True)
        return ((g - m) / jnp.sqrt(s + eps)).reshape(v.shape)

    def _ln_c(v, eps=1e-6):
        m = jnp.mean(v, axis=-1, keepdims=True)
        s = jnp.var(v, axis=-1, keepdims=True)
        return (v - m) / jnp.sqrt(s + eps)

    def _ln_t(v, eps=1e-5):
        m = jnp.mean(v, axis=-1, keepdims=True)
        s = jnp.var(v, axis=-1, keepdims=True)
        return (v - m) / jnp.sqrt(s + eps)

    def _to_tokens(v):
        B_, H_, W_, C_ = v.shape
        return v.reshape(B_, H_ * W_, C_)
    def _from_tokens(t, like):
        return t.reshape(like.shape)

    x = x + _L0_conv_ref(_gn(x), L0_conv_conv, L0_conv_skip_kernel, L0_conv_skip_bias)
    x = x + _L1_conv_ref(_gn(x), L1_conv_fw1, L1_conv_fw2, L1_conv_W, L1_conv_b)
    return x


_drawn_inputs = setup_inputs


def setup_inputs(seed=0):
    import zlib

    import numpy as np

    out = dict(_drawn_inputs(seed))
    spreads = {'L1_conv_b': (0.0, 0.1)}
    factors = {'L0_conv_conv': 200.0, 'L1_conv_fw1': 200.0, 'L1_conv_fw2': 200.0, 'L1_conv_W': 200.0}
    for name, (base, spread) in spreads.items():
        noise = np.random.default_rng([zlib.crc32(name.encode()), seed]).standard_normal(out[name].shape)
        drawn = base * np.exp(spread * noise) if base else spread * noise
        out[name] = jnp.asarray(drawn.astype(out[name].dtype))
    for name, factor in factors.items():
        out[name] = (out[name] * factor).astype(out[name].dtype)
    return out
```

```python
from contextlib import ExitStack

import numpy as np

import concourse.bass as bass
from concourse import mybir

F32 = mybir.dt.float32
F16 = mybir.dt.float16
ALU = mybir.AluOpType
ACT = mybir.ActivationFunctionType
AX = mybir.AxisListType

N = 256
C = 64
P = 128
HALVES = N // P
K0 = 16
K1 = 32
KX = 2 * K1
EPS = 1e-5

CW = 16
SLOTS = 4
CPH = HALVES * P // CW
CG = 8
GROUPS = C // CG
ROW_BANKS = 4


class Memory:

    def __init__(self, nc):
        self.nc, self.stack = nc, ExitStack()

    def sb(self, name, shape, dt=F32):
        return self.stack.enter_context(self.nc.sbuf_tensor(name, shape, dt))

    def ps(self, name, shape, dt=F32):
        return self.stack.enter_context(self.nc.psum_tensor(name, shape, dt))

    def sem(self, name):
        return self.stack.enter_context(self.nc.semaphore(name))

    def __enter__(self):
        return self

    def __exit__(self, *e):
        return self.stack.__exit__(*e)


def load_constants(nc, pairs):
    with Memory(nc) as m:
        landed = m.sem("constants_landed")
        with nc.Block() as block:
            @block.sync
            def _(sp):
                for dst, src in pairs:
                    sp.dma_start(dst, src).then_inc(landed, 16)
                sp.wait_ge(landed, 16 * len(pairs))


def pass_1(nc, B, x, modes_x, gram, rows_dft, cols_dft):
    with Memory(nc) as m:
        stage = [m.sb(f"stage{s}", [P, CW, C]) for s in range(SLOTS)]
        parts = [m.sb(f"parts{i}", [P, HALVES, P, 2 * C], F16) for i in range(2)]
        rows = m.sb("rows", [P, HALVES, 2, 2, K1, C], F16)
        modes = m.sb("modes", [P, K1 // 2, 2 * K1])
        row_ps = [m.ps(f"row_ps{i}", [P, CG, 2 * K1]) for i in range(ROW_BANKS)]
        gram_ps = m.ps("gram_ps", [P, 512])
        mode_ps = [m.ps(f"mode_ps{i}", [P, K1 // 4, 2 * K1]) for i in range(2)]

        landed = [m.sem(f"chunk_landed{s}") for s in range(SLOTS)]
        high_done = m.sem("high_done")
        split_done = m.sem("split_done")
        half_used = m.sem("half_used")
        gram_ready = m.sem("gram_ready")
        gram_taken = m.sem("gram_taken")
        rows_ready = m.sem("rows_ready")
        rows_high = m.sem("rows_high")
        rows_taken = m.sem("rows_taken")
        modes_ready = m.sem("modes_ready")
        modes_taken = m.sem("modes_taken")
        modes_stored = m.sem("modes_stored")

        block = m.stack.enter_context(nc.Block())

        @block.sync
        def _(sp):
            with sp.Fori(0, B) as b:
                for wh in range(HALVES):
                    for k in range(CPH):
                        hh, w0 = divmod(k * CW, P)
                        c = wh * CPH + k
                        sp.wait_ge(split_done, b * (2 * CPH) + c + 1)
                        sp.dma_start(
                            stage[c % SLOTS][:, :, :],
                            x[bass.ds(b, 1), hh * P:(hh + 1) * P, wh * P + w0:wh * P + w0 + CW, :]
                            .rearrange("o h w c -> h (o w) c"),
                        ).then_inc(landed[c % SLOTS], 16)

        def chunk_parts(c):
            wh, k = divmod(c, CPH)
            hh, w0 = divmod(k * CW, P)
            t = parts[wh][:, hh, w0:w0 + CW, :]
            return t[:, :, 0:C], t[:, :, C:2 * C]

        def row_slot(wh, g):
            return [rows[:, wh, p, :, :, g * CG:(g + 1) * CG].rearrange("w r k c -> w c (r k)")
                    for p in range(2)]

        @block.scalar
        def _(act):
            def high(b, c):
                if c % CPH == 0:
                    act.wait_ge(half_used, 2 * b + c // CPH + 1)
                act.wait_ge(landed[c % SLOTS], 16 * (b * (2 * CPH // SLOTS) + c // SLOTS + 1))
                nc.scalar.activation(chunk_parts(c)[0], stage[c % SLOTS][:, :, :], ACT.Copy).then_inc(high_done, 1)

            def image(b, last):
                for wh in range(HALVES):
                    for g in range(GROUPS):
                        act.wait_ge(rows_ready, (b * HALVES + wh) * GROUPS + g + 1)
                        nc.scalar.activation(row_slot(wh, g)[0], row_ps[g % ROW_BANKS][:, :, :],
                                             ACT.Copy, scale=1 / 16).then_inc(rows_high, 1)
                        for j in range(CPH // GROUPS):
                            c = (wh + 1) * CPH + g * CPH // GROUPS + j
                            if c < 2 * CPH:
                                high(b, c)
                            elif not last:
                                high(b + 1, c - 2 * CPH)
                act.wait_ge(modes_ready, 2 * b + 1)
                act.wait_ge(modes_stored, 32 * b + 1)
                nc.scalar.activation(modes[:, 0:K1 // 4, :], mode_ps[0][:, :, :], ACT.Copy,
                                     scale=1 / 16).then_inc(modes_taken, 1)
                act.wait_ge(modes_taken, 2 * b + 4)
                for q in range(2):
                    dst = modes_x[b:b + 1] if last else modes_x[bass.ds(b, 1), :, :, :, :]
                    act.dma_start(dst.rearrange("o c (k q) r y -> q c (o k) (r y)", q=2)[q],
                                  modes[q * C:(q + 1) * C, :, :]).then_inc(modes_stored, 16)

            act.sem_inc(modes_stored, 1)
            for c in range(CPH):
                high(0, c)
            with act.Fori(0, B - 1) as b:
                image(b, False)
            image(B - 1, True)
            act.wait_ge(modes_stored, 32 * B + 1)

        @block.vector
        def _(dve):
            dve.sem_inc(split_done, SLOTS)
            dve.sem_inc(gram_taken, 1)
            dve.sem_inc(rows_taken, ROW_BANKS)
            dve.sem_inc(modes_taken, 2)

            def low(b, c):
                dve.wait_ge(high_done, b * (2 * CPH) + c + 1)
                hi, lo = chunk_parts(c)
                nc.vector.tensor_tensor(lo, stage[c % SLOTS][:, :, :], hi, ALU.subtract).then_inc(split_done, 1)

            def image(b, last):
                for wh in range(HALVES):
                    for g in range(GROUPS):
                        n = (b * HALVES + wh) * GROUPS + g + 1
                        dve.wait_ge(rows_high, n)
                        hi, lo = row_slot(wh, g)
                        nc.vector.scalar_tensor_tensor(out=lo, in0=row_ps[g % ROW_BANKS][:, :, :], scalar=1 / 16,
                                                       in1=hi, op0=ALU.mult, op1=ALU.subtract).then_inc(rows_taken, 1)
                        for j in range(CPH // GROUPS):
                            c = (wh + 1) * CPH + g * CPH // GROUPS + j
                            if c < 2 * CPH:
                                low(b, c)
                            elif not last:
                                low(b + 1, c - 2 * CPH)
                        if wh == 1 and g == 0:
                            dve.wait_ge(gram_ready, b + 1)
                            nc.vector.tensor_copy(gram[:, bass.ds(b, 1), :].rearrange("p o c -> p (o c)"),
                                                  gram_ps[:, 0:C]).then_inc(gram_taken, 1)
                dve.wait_ge(modes_ready, 2 * b + 2)
                dve.wait_ge(modes_stored, 32 * b + 1)
                nc.vector.tensor_scalar(modes[:, K1 // 4:, :], mode_ps[1][:, :, :], 1 / 16, None,
                                        ALU.mult).then_inc(modes_taken, 1)

            for c in range(CPH):
                low(0, c)
            with dve.Fori(0, B - 1) as b:
                image(b, False)
            image(B - 1, True)

        @block.tensor
        def _(pe):
            pe.sem_inc(half_used, 2)
            with pe.Fori(0, B) as b:
                for wh in range(HALVES):
                    if wh == 0:
                        pe.wait_ge(gram_taken, b + 1)
                    for k in range(CPH):
                        hh, w0 = divmod(k * CW, P)
                        pe.wait_ge(split_done, b * (2 * CPH) + SLOTS + wh * CPH + k + 1)
                        for w in range(w0, w0 + CW):
                            col = parts[wh][:, hh, w, :]
                            last = nc.tensor.matmul(gram_ps[:, 0:C], col, col[:, 0:C],
                                                    start=(wh == 0 and k == 0 and w == w0),
                                                    stop=(wh == 1 and k == CPH - 1 and w == w0 + CW - 1))
                    if wh == 1:
                        last.then_inc(gram_ready, 1)
                    for g in range(GROUPS):
                        pe.wait_ge(rows_taken, (b * HALVES + wh) * GROUPS + g + 1)
                        for c in range(CG):
                            n = 0
                            for hh in range(HALVES):
                                for p, q in ((0, 0), (0, 1), (1, 0)):
                                    last = nc.tensor.matmul(
                                        row_ps[g % ROW_BANKS][:, c, :], parts[wh][:, hh, :, p * C + g * CG + c],
                                        rows_dft[:, hh, q, :], start=(n == 0), stop=(n == 5))
                                    n += 1
                        last.then_inc(rows_ready, 1)
                    pe.sem_inc(half_used, 1)
                pe.wait_ge(rows_taken, (b + 1) * HALVES * GROUPS + ROW_BANKS)
                for i in range(2):
                    pe.wait_ge(modes_taken, 2 * b + i + 1)
                    for j in range(K1 // 4):
                        kx = 2 * (i * K1 // 4 + j)
                        n = 0
                        for wh in range(HALVES):
                            for ri in range(2):
                                for p, q in ((0, 0), (0, 1), (1, 0)):
                                    last = nc.tensor.matmul(
                                        mode_ps[i][:, j, :], rows[:, wh, p, ri, kx:kx + 2, :],
                                        cols_dft[:, wh, q, ri, :], start=(n == 0), stop=(n == 11))
                                    n += 1
                    last.then_inc(modes_ready, 1)


def norm_0(nc, B, gram, apply, modes_x, planes_0, x1_modes, w):
    MODES = K0 * K0
    MC = 64
    MB = 32
    xm = x1_modes
    with Memory(nc) as m:
        products = m.sb("products", [P, B, C])
        scratch = m.sb("scratch", [P, B, C])
        sums = m.sb("sums", [P, 2, B])
        means = m.sb("means", [P, 2, B])
        var = m.sb("var", [P, B])
        std = m.sb("std", [P, B])
        rstd = m.sb("rstd", [P, B])
        shift = m.sb("shift", [P, B])
        A = m.sb("A", [P, B, C])
        const = m.sb("const", [C, B])
        mixed_in = m.sb("mixed_in", [P, MODES, 2, B])
        weights = [m.sb(f"weights{i}", [P, MC, C]) for i in range(2)]
        S = m.sb("S", [C, B, 2, K0, K0])
        S_weighted = m.sb("S_weighted", [C, B, 2, K0, K0])
        S_real = m.sb("S_real", [C, B, 2, K0, K0])
        cross = m.sb("cross", [C, 2, K0, K0])
        cross_sum = m.sb("cross_sum", [C, B])
        planes = [m.sb(f"planes{i}", [P, 3, C]) for i in range(2)]

        ps_products = m.ps("ps_products", [P, 512])
        ps_small = m.ps("ps_small", [P, 512])
        ps_mix = [m.ps(f"ps_mix{i}", [P, 512]) for i in range(2)]
        ps_apply = [m.ps(f"ps_apply{i}", [P, 512]) for i in range(2)]
        ps_plane = [m.ps(f"ps_plane{i}", [P, 3, C]) for i in range(2)]

        modes_landed = m.sem("modes_landed")
        weights_landed = [m.sem(f"weights_landed{i}") for i in range(2)]
        products_ready = m.sem("products_ready")
        sums_ready = m.sem("sums_ready")
        means_ready = m.sem("means_ready")
        var_ready = m.sem("var_ready")
        std_ready = m.sem("std_ready")
        shift_ready = m.sem("shift_ready")
        const_ready = m.sem("const_ready")
        A_ready = m.sem("A_ready")
        input_ready = m.sem("input_ready")
        mix_ready = m.sem("mix_ready")
        mix_taken = m.sem("mix_taken")
        S_ready = m.sem("S_ready")
        U_ready = m.sem("U_ready")
        U_taken = m.sem("U_taken")
        GA_ready = m.sem("GA_ready")
        AGA_ready = m.sem("AGA_ready")
        square_ready = m.sem("square_ready")
        plane_ready = m.sem("plane_ready")
        plane_taken = m.sem("plane_taken")
        plane_stored = [m.sem(f"plane_stored{i}") for i in range(2)]
        x1_ready = m.sem("x1_ready")
        x1_copied = m.sem("x1_copied")
        chain = m.sem("vector_chain")

        block = m.stack.enter_context(nc.Block())
        BANKS = MODES // MB

        @block.sync
        def _(sp):
            for b in range(B):
                for d in range(2):
                    sp.dma_start(xm[d * C:(d + 1) * C, b, :, :, :], modes_x[b]).then_inc(modes_landed, 16)
            for k in range(MODES // MC):
                if k >= 2:
                    sp.wait_ge(mix_ready, (k - 1) * MC // MB)
                for r in range(2):
                    sp.dma_start(
                        weights[k % 2][r * C:(r + 1) * C, :, :],
                        w["conv"][r].rearrange("x y i o -> i (x y) o")[:, k * MC:(k + 1) * MC, :],
                    ).then_inc(weights_landed[k % 2], 16)
            sp.wait_ge(x1_ready, 1)
            sp.dma_start(xm[C:2 * C, :, :, :, :], xm[0:C, :, :, :, :]).then_inc(x1_copied, 16)
            sp.wait_ge(x1_copied, 16)

        @block.gpsimd
        def _(pool):
            for n in range(2 * B):
                b, q = divmod(n, 2)
                pool.wait_ge(plane_taken, n + 1)
                pool.dma_start(
                    planes_0[b, :, q * (K0 // 2):(q + 1) * (K0 // 2), :, :].rearrange("p x y c -> (x y) p c"),
                    planes[n % 2][:, :, :]).then_inc(plane_stored[n % 2], 16)
            for i in range(2):
                pool.wait_ge(plane_stored[i], 16 * B)

        @block.scalar
        def _(act):
            for n in range(2):
                act.wait_ge(var_ready, n + 1)
                nc.scalar.activation(std[0:P >> n, :], var[0:P >> n, :], ACT.Sqrt).then_inc(std_ready, 1)
                if n == 1:
                    break
                for t in range(4 * B):
                    b, q = divmod(t, 4)
                    act.wait_ge(U_ready, t + 1)
                    nc.scalar.activation(xm[0:C, b, :, :, :].rearrange("c x r y -> c (x r y)")[:, q * 512:(q + 1) * 512],
                                         ps_apply[t % 2][0:C, :], ACT.Copy).then_inc(U_taken, 1)
                for t in range(2 * B):
                    act.wait_ge(plane_ready, t + 1)
                    if t >= 2:
                        act.wait_ge(plane_stored[t % 2], 16 * (t // 2))
                    nc.scalar.activation(planes[t % 2][:, :, :], ps_plane[t % 2][:, :, :],
                                         ACT.Copy).then_inc(plane_taken, 1)

        @block.vector
        def _(dve):
            count = [0]

            def step(ins):
                count[0] += 1
                ins.then_inc(chain, 1)
                dve.wait_ge(chain, count[0])

            def norm(n, rows):
                dve.wait_ge(means_ready, n + 1)
                step(nc.vector.tensor_copy(means[0:rows, :, :].rearrange("p s b -> p (s b)"), ps_small[0:rows, 0:2 * B]))
                step(nc.vector.tensor_tensor(var[0:rows, :], means[0:rows, 0, :], means[0:rows, 0, :], ALU.mult))
                step(nc.vector.tensor_tensor(var[0:rows, :], means[0:rows, 1, :], var[0:rows, :], ALU.subtract))
                nc.vector.tensor_scalar(var[0:rows, :], var[0:rows, :], 0.0, EPS, ALU.max, ALU.add).then_inc(var_ready, 1)
                dve.wait_ge(std_ready, n + 1)
                step(nc.vector.reciprocal(rstd[0:rows, :], std[0:rows, :]))
                step(nc.vector.tensor_tensor(std[0:rows, :], rstd[0:rows, :], rstd[0:rows, :], ALU.mult))
                step(nc.vector.tensor_tensor(std[0:rows, :], std[0:rows, :], var[0:rows, :], ALU.mult))
                step(nc.vector.tensor_scalar(std[0:rows, :], std[0:rows, :], -0.5, 1.5, ALU.mult, ALU.add))
                step(nc.vector.tensor_tensor(rstd[0:rows, :], rstd[0:rows, :], std[0:rows, :], ALU.mult))
                nc.vector.scalar_tensor_tensor(out=shift[0:rows, :], in0=means[0:rows, 0, :], scalar=-1.0,
                                               in1=rstd[0:rows, :], op0=ALU.mult, op1=ALU.mult).then_inc(shift_ready, 1)
                dve.wait_ge(shift_ready, n + 1)

            dve.wait_ge(products_ready, 1)
            step(nc.vector.tensor_copy(products[:, :, :].rearrange("p b c -> p (b c)"), ps_products[:, 0:B * C]))
            for b in range(B):
                nc.vector.tensor_tensor(scratch[:, b, :], products[:, b, :], w["eye_twice"][:, :], ALU.mult)
            step(nc.vector.memset(apply[:, :, :, :], 0.0))
            step(nc.vector.tensor_reduce(sums[:, 1, :], scratch[:, :, :], AX.X, ALU.add))
            step(nc.vector.tensor_scalar(sums[:, 1, :], sums[:, 1, :], 1 / N / N, None, ALU.mult))
            dve.wait_ge(modes_landed, 32 * B)
            nc.vector.tensor_scalar(sums[:, 0, :], xm[:, :, 0, 0, 0], 1 / N, None, ALU.mult).then_inc(sums_ready, 1)
            norm(0, P)
            for b in range(B):
                ins = nc.vector.scalar_tensor_tensor(out=A[:, b, :], in0=w["skip"][:, :], scalar=rstd[:, b:b + 1],
                                                     in1=w["eye_twice"][:, :], op0=ALU.mult, op1=ALU.add)
            ins.then_inc(A_ready, 1)
            for b in range(B):
                for d in range(2):
                    rows = slice(d * C, (d + 1) * C)
                    for r in range(2):
                        src = xm[rows, b, 0:K0, r if d == 0 else 1 - r, 0:K0]
                        dst = mixed_in[rows, :, r, b].rearrange("p (x y) -> p x y", x=K0)
                        nc.vector.tensor_scalar(dst, src, rstd[rows, b:b + 1], -1.0 if (d, r) == (1, 0) else 1.0,
                                                ALU.mult, ALU.mult)
            dve.wait_ge(const_ready, 1)
            step(nc.vector.tensor_scalar(const[:, :], ps_small[0:C, 64:64 + B], w["skip_bias"][:, 0:1], float(N),
                                         ALU.add, ALU.mult))
            for d in range(2):
                rows = slice(d * C, (d + 1) * C)
                ins = nc.vector.scalar_tensor_tensor(out=mixed_in[rows, 0, d, :], in0=shift[rows, :], scalar=float(N),
                                                     in1=mixed_in[rows, 0, d, :], op0=ALU.mult, op1=ALU.add)
                step(ins)
            dve.sem_inc(input_ready, 1)
            for d in range(2):
                rows = slice(d * C, (d + 1) * C)
                step(nc.vector.tensor_scalar(apply[rows, :, 0, rows], A[rows, :, :], 16.0, None, ALU.mult))
                for b in range(B):
                    nc.vector.scalar_tensor_tensor(out=apply[rows, b, 1, rows], in0=A[rows, b, :], scalar=16.0,
                                                   in1=apply[rows, b, 0, rows], op0=ALU.mult, op1=ALU.subtract)
            dve.wait_ge(GA_ready, 1)
            nc.vector.tensor_tensor(scratch[0:C, :, :].rearrange("p b c -> p (b c)"), ps_products[0:C, 0:B * C],
                                    A[0:C, :, :].rearrange("p b c -> p (b c)"), ALU.mult).then_inc(AGA_ready, 1)
            for t in range(BANKS):
                dve.wait_ge(mix_ready, t + 1)
                v = ps_mix[t % 2][0:C, 0:MB * 2 * B].rearrange("p (k r b) -> p k r b", r=2, b=B)
                for r in range(2):
                    for x0 in range(MB // K0):
                        ins = nc.vector.tensor_copy(S[:, :, r, t * MB // K0 + x0, :],
                                                    v[:, x0 * K0:(x0 + 1) * K0, r, :].rearrange("p k b -> p b k"))
                ins.then_inc(mix_taken, 1)
            dve.wait_ge(mix_taken, BANKS)
            nc.vector.tensor_tensor(S[:, :, 0, 0, 0], S[:, :, 0, 0, 0], const[:, :], ALU.add).then_inc(S_ready, 1)
            dve.wait_ge(S_ready, 1)

            def flat(t):
                return t[:, :, :, :, :].rearrange("p b r x y -> p (b r x y)")
            step(nc.vector.tensor_scalar(flat(S_weighted), flat(S), 2.0, None, ALU.mult))
            step(nc.vector.tensor_copy(S_weighted[:, :, :, :, 0], S[:, :, :, :, 0]))
            step(nc.vector.tensor_scalar(flat(S_real), flat(S_weighted), 0.5, None, ALU.mult))
            nc.vector.tensor_copy(S_real[:, :, 0, 0, 0], S[:, :, 0, 0, 0])
            step(nc.vector.memset(S_real[:, :, 1, 0, 0], 0.0))
            dve.wait_ge(U_taken, 4 * B)
            for b in range(B):
                for r in range(2):
                    step(nc.vector.scalar_tensor_tensor(out=cross[:, r, :, :], in0=xm[0:C, b, 0:K0, r, 0:K0], scalar=2.0,
                                                        in1=S_real[:, b, r, :, :], op0=ALU.mult, op1=ALU.add))
                    nc.vector.tensor_tensor(xm[0:C, b, 0:K0, r, 0:K0], xm[0:C, b, 0:K0, r, 0:K0],
                                            S_real[:, b, r, :, :], ALU.add)
                products_of_modes = cross[:, :, :, :].rearrange("p r x y -> p (r x y)")
                step(nc.vector.tensor_tensor(products_of_modes, products_of_modes,
                                             S_weighted[:, b, :, :, :].rearrange("p r x y -> p (r x y)"), ALU.mult))
                step(nc.vector.tensor_reduce(cross_sum[:, b:b + 1], products_of_modes, AX.X, ALU.add))
            dve.wait_ge(square_ready, 1)
            step(nc.vector.tensor_tensor(cross_sum[:, :], cross_sum[:, :], ps_small[0:C, 128:128 + B], ALU.add))
            nc.vector.tensor_scalar(sums[0:C, 0, :], xm[0:C, :, 0, 0, 0], 1 / N, None, ALU.mult).then_inc(sums_ready, 1)
            nc.vector.tensor_scalar(sums[0:C, 1, :], cross_sum[:, :], 1 / N / N, None, ALU.mult).then_inc(sums_ready, 1)
            norm(1, C)
            for b in range(B):
                v = xm[0:C, b, :, :, :].rearrange("p x r y -> p (x r y)")
                ins = nc.vector.tensor_scalar(v, v, rstd[0:C, b:b + 1], None, ALU.mult)
            step(ins)
            nc.vector.scalar_tensor_tensor(out=xm[0:C, :, 0, 0, 0], in0=shift[0:C, :], scalar=float(N),
                                           in1=xm[0:C, :, 0, 0, 0], op0=ALU.mult, op1=ALU.add).then_inc(x1_ready, 1)

        @block.tensor
        def _(pe):
            nc.tensor.matmul(ps_products[:, 0:B * C], w["sum_parts"][:, :],
                             gram[:, :, :].rearrange("p b c -> p (b c)"), start=True, stop=True).then_inc(products_ready, 1)
            pe.wait_ge(sums_ready, 1)
            nc.tensor.matmul(ps_small[:, 0:2 * B], w["pair_mean"][:, :], sums[:, :, :].rearrange("p s b -> p (s b)"),
                             start=True, stop=True).then_inc(means_ready, 1)
            pe.wait_ge(shift_ready, 1)
            nc.tensor.matmul(ps_small[0:C, 64:64 + B], w["skip"][0:C, :], shift[0:C, :],
                             start=True, stop=True).then_inc(const_ready, 1)
            pe.wait_ge(A_ready, 1)
            for b in range(B):
                last = nc.tensor.matmul(ps_products[0:C, b * C:(b + 1) * C], products[0:C, b, :], A[0:C, b, :],
                                        start=True, stop=True)
            last.then_inc(GA_ready, 1)
            pe.wait_ge(input_ready, 1)
            for t in range(BANKS):
                k = t * MB // MC
                if t * MB % MC == 0:
                    pe.wait_ge(weights_landed[k % 2], 32 * (k // 2 + 1))
                if t >= 2:
                    pe.wait_ge(mix_taken, t - 1)
                for j in range(MB):
                    mode = t * MB + j
                    last = nc.tensor.matmul(ps_mix[t % 2][0:C, j * 2 * B:(j + 1) * 2 * B],
                                            weights[k % 2][:, mode % MC, :],
                                            mixed_in[:, mode, :, :].rearrange("p r b -> p (r b)"),
                                            start=True, stop=True)
                last.then_inc(mix_ready, 1)
            for t in range(4 * B):
                b, q = divmod(t, 4)
                if t >= 2:
                    pe.wait_ge(U_taken, t - 1)
                nc.tensor.matmul(ps_apply[t % 2][0:C, :], A[0:C, b, :],
                                 xm[0:C, b, :, :, :].rearrange("c x r y -> c (x r y)")[:, q * 512:(q + 1) * 512],
                                 start=True, stop=True).then_inc(U_ready, 1)
            pe.wait_ge(AGA_ready, 1)
            for b in range(B):
                last = nc.tensor.matmul(ps_small[0:C, 128 + b:129 + b], scratch[0:C, b, :], w["ones"][0:C, 0:1],
                                        start=True, stop=True)
            last.then_inc(square_ready, 1)
            pe.wait_ge(S_ready, 1)
            for t in range(2 * B):
                b, q = divmod(t, 2)
                if t >= 2:
                    pe.wait_ge(plane_taken, t - 1)
                for plane, (r, eye) in enumerate(((0, "eye"), (1, "eye"), (0, "minus_eye"))):
                    src = S[:, b, r, q * (K0 // 2):(q + 1) * (K0 // 2), :].rearrange("c x y -> c (x y)")
                    last = nc.tensor.matmul(ps_plane[t % 2][:, plane, :], src, w[eye][0:C, 0:C], start=True, stop=True)
                last.then_inc(plane_ready, 1)
            pe.wait_ge(sums_ready, 3)
            nc.tensor.matmul(ps_small[0:C, 0:2 * B], w["pair_mean"][0:C, 0:C], sums[0:C, :, :].rearrange("p s b -> p (s b)"),
                             start=True, stop=True).then_inc(means_ready, 1)


def mixing_1(nc, B, x1_modes, fw, mixed):
    KC = 2
    SL = 2
    MG = K1 // 4
    R = 2 * 2 * B
    with Memory(nc) as m:
        weights = [m.sb(f"fw{i}", [P, C, KC, 2 * K1]) for i in range(SL)]
        blocks = [m.sb(f"blocks{i}", [P, 2, B, 2, K1]) for i in range(2)]
        out = [m.sb(f"mix_out{i}", [P, MG, 2 * C]) for i in range(2)]
        ps = [[m.ps(f"mix_ps{i}{h}", [P, MG // 2, 2 * C]) for h in range(2)] for i in range(2)]

        landed = [m.sem(f"fw_landed{i}") for i in range(SL)]
        zeroed = m.sem("zeroed")
        placed = m.sem("placed")
        ready = m.sem("mix1_ready")
        taken_low = m.sem("mix1_taken_low")
        taken_high = m.sem("mix1_taken_high")
        stored = [m.sem(f"mix1_stored{i}") for i in range(2)]
        block = m.stack.enter_context(nc.Block())

        @block.sync
        def _(sp):
            for k in range(K1 // KC):
                if k >= SL:
                    sp.wait_ge(ready, (k - SL + 1) * KC)
                for f in range(2):
                    sp.dma_start(weights[k % SL][f * C:(f + 1) * C, :, :, :].rearrange("i o x y -> i o (x y)"),
                                 fw[f].rearrange("i o x y r -> i o (x y r)")[:, :, k * KC * 2 * K1:(k + 1) * KC * 2 * K1],
                                 ).then_inc(landed[k % SL], 16)

        @block.gpsimd
        def _(pool):
            for i in range(2):
                nc.gpsimd.memset(blocks[i][:, :, :, :, :], 0.0).then_inc(zeroed, 1)
            pool.wait_ge(zeroed, 2)
            for x in range(K1):
                if x >= 2:
                    pool.wait_ge(ready, x - 1)
                for f in range(2):
                    rows = slice(f * C, (f + 1) * C)
                    nc.gpsimd.tensor_copy(blocks[x % 2][rows, f, :, :, :].rearrange("p b r y -> p b (r y)"),
                                          x1_modes[rows, :, x, :, :].rearrange("p b r y -> p b (r y)")).then_inc(placed, 1)

        @block.tensor
        def _(pe):
            for x in range(K1):
                k = x // KC
                if x % KC == 0:
                    pe.wait_ge(landed[k % SL], 32 * (k // SL + 1))
                pe.wait_ge(placed, 2 * (x + 1))
                if x >= 2:
                    pe.wait_ge(taken_low, x - 1)
                    pe.wait_ge(taken_high, x - 1)
                for j in range(4):
                    for g in range(MG):
                        y = MG * j + g
                        last = nc.tensor.matmul(
                            ps[x % 2][g // (MG // 2)][32 * j:32 * j + R, g % (MG // 2), :],
                            blocks[x % 2][:, :, :, :, y].rearrange("p f b r -> p (f b r)"),
                            weights[k % SL][:, :, x % KC, 2 * y:2 * y + 2],
                            start=True, stop=True, tile_position=(0, 32 * j))
                last.then_inc(ready, 1)

        @block.scalar
        def _(act):
            for x in range(K1):
                act.wait_ge(ready, x + 1)
                if x >= 2:
                    act.wait_ge(stored[x % 2], 64 * (x // 2))
                for j in range(4 if R < 32 else 1):
                    rows = slice(32 * j, 32 * j + R) if R < 32 else slice(0, P)
                    last = nc.scalar.activation(out[x % 2][rows, 0:MG // 2, :], ps[x % 2][0][rows, :, :], ACT.Copy)
                last.then_inc(taken_low, 1)
                act.wait_ge(taken_low, x + 1)
                act.wait_ge(taken_high, x + 1)
                for j in range(4):
                    act.dma_start(
                        mixed.rearrange("f b r x y w -> (f b r) x (y w)")[:, x, j * MG * 2 * C:(j + 1) * MG * 2 * C],
                        out[x % 2][32 * j:32 * j + R, :, :].rearrange("p g w -> p (g w)")).then_inc(stored[x % 2], 16)
            for i in range(2):
                act.wait_ge(stored[i], 64 * (K1 // 2))

        @block.vector
        def _(dve):
            for x in range(K1):
                dve.wait_ge(ready, x + 1)
                if x >= 2:
                    dve.wait_ge(stored[x % 2], 64 * (x // 2))
                for j in range(4 if R < 32 else 1):
                    rows = slice(32 * j, 32 * j + R) if R < 32 else slice(0, P)
                    last = nc.vector.tensor_copy(out[x % 2][rows, MG // 2:, :], ps[x % 2][1][rows, :, :])
                last.then_inc(taken_high, 1)


def project_1(nc, B, mixed, planes_1, w):
    Q = KX // 4
    STEP = 4
    SCALE = 1.0 / (N * float(np.sqrt(np.float32(N * (N // 2 + 1)))))
    with Memory(nc) as m:
        raw = [m.sb(f"raw{i}", [P, 2, 2, Q // 2, C, 2]) for i in range(2)]
        modes = m.sb("complex", [P, Q, 2, C])
        turned = [m.sb(f"turned{i}", [P, STEP, P]) for i in range(2)]
        planes = [m.sb(f"planes1{i}", [P, Q, 3, C]) for i in range(2)]
        ps_turn = [m.ps(f"ps_turn{i}", [P, STEP, P]) for i in range(2)]
        ps_out = [m.ps(f"ps_out{i}", [P, 2, 3, C]) for i in range(4)]

        landed = [m.sem(f"raw_landed{i}") for i in range(2)]
        combined = m.sem("combined")
        modes_used = m.sem("complex_used")
        turn_ready = m.sem("turn_ready")
        turn_taken = m.sem("turn_taken")
        out_ready = m.sem("out_ready")
        out_taken = m.sem("out_taken")
        biased = m.sem("biased")
        stored = [m.sem(f"planes1_stored{i}") for i in range(2)]
        block = m.stack.enter_context(nc.Block())

        @block.sync
        def _(sp):
            for b in range(B):
                if b >= 2:
                    sp.wait_ge(combined, 4 * (b - 1))
                for f in range(2):
                    for r in range(2):
                        sp.dma_start(
                            raw[b % 2][:, f, r, :, :, :].rearrange("p k o w -> p k (o w)"),
                            mixed[f, b, r].rearrange("(k x) y w -> (x y) k w", x=4)).then_inc(landed[b % 2], 16)

        @block.vector
        def _(dve):
            for b in range(B):
                dve.wait_ge(landed[b % 2], 64 * (b // 2 + 1))
                if b >= 1:
                    dve.wait_ge(turn_ready, b * Q // STEP)
                for f in range(2):
                    v = raw[b % 2]
                    out = modes[:, f * Q // 2:(f + 1) * Q // 2, :, :]
                    nc.vector.tensor_tensor(out[:, :, 0, :], v[:, f, 0, :, :, 0], v[:, f, 1, :, :, 1],
                                            ALU.subtract).then_inc(combined, 1)
                    nc.vector.tensor_tensor(out[:, :, 1, :], v[:, f, 0, :, :, 1], v[:, f, 1, :, :, 0],
                                            ALU.add).then_inc(combined, 1)
                for s in range(Q // STEP):
                    n = b * Q // STEP + s
                    dve.wait_ge(turn_ready, n + 1)
                    if n >= 2:
                        dve.wait_ge(out_ready, 2 * (n - 1))
                    nc.vector.tensor_copy(turned[n % 2][:, :, :], ps_turn[n % 2][:, :, :]).then_inc(turn_taken, 1)
                dve.wait_ge(out_taken, (b + 1) * Q // 2)
                for plane, op in ((0, ALU.add), (2, ALU.subtract)):
                    at = planes[b % 2][0:1, 0, plane, :]
                    nc.vector.tensor_tensor(at, at, w["bias_n"][0:1, :], op).then_inc(biased, 1)

        @block.tensor
        def _(pe):
            for b in range(B):
                pe.wait_ge(combined, 4 * (b + 1))
                for s in range(Q // STEP):
                    n = b * Q // STEP + s
                    if n >= 2:
                        pe.wait_ge(turn_taken, n - 1)
                    for j in range(STEP):
                        last = nc.tensor.transpose(ps_turn[n % 2][:, j, :],
                                                   modes[:, s * STEP + j, :, :].rearrange("p r c -> p (r c)"),
                                                   w["eye"][:, :])
                    last.then_inc(turn_ready, 1)
                    pe.wait_ge(turn_taken, n + 1)
                    for h in range(2):
                        i = 2 * n + h
                        if i >= 4:
                            pe.wait_ge(out_taken, i - 3)
                        for j in range(2):
                            last = nc.tensor.matmul(ps_out[i % 4][:, j, :, :].rearrange("p a c -> p (a c)"),
                                                    turned[n % 2][:, 2 * h + j, :], w["project"][:, :],
                                                    start=True, stop=True)
                        last.then_inc(out_ready, 1)

        @block.scalar
        def _(act):
            for b in range(B):
                if b >= 2:
                    act.wait_ge(stored[b % 2], 48 * (b // 2))
                for h in range(Q // 2):
                    i = b * Q // 2 + h
                    act.wait_ge(out_ready, i + 1)
                    nc.scalar.activation(planes[b % 2][:, 2 * h:2 * h + 2, :, :], ps_out[i % 4][:, :, :, :],
                                         ACT.Copy, scale=SCALE).then_inc(out_taken, 1)

        @block.gpsimd
        def _(pool):
            for b in range(B):
                pool.wait_ge(biased, 2 * (b + 1))
                for plane in range(3):
                    pool.dma_start(
                        planes_1[b, plane].rearrange("(k x) y c -> (x y) k c", x=4),
                        planes[b % 2][:, :, plane, :]).then_inc(stored[b % 2], 16)
            for i in range(min(B, 2)):
                pool.wait_ge(stored[i], 48 * ((B - i + 1) // 2))


W2 = 32
UW = 8
UNITS = W2 // UW
CHUNKS = HALVES * N // W2
X_SLOTS = 4
Y_SLOTS = 2
D_ROWS = 16
D1 = 2 * KX // D_ROWS
DC = D1 + 2 * K0 // D_ROWS


def pass_2(nc, B, x, y, apply, planes_0, planes_1, w):
    with Memory(nc) as m:
        stage = [m.sb(f"plane_stage{i}", [P, D_ROWS, C]) for i in range(2)]
        D = [m.sb("planes_s", [4 * K0, 4, 2 * K0, C], F16), m.sb("planes_t", [4 * K1, 2 * KX, C], F16)]
        cols_0 = m.sb("cols_0", [P, N, C], F16)
        cols_1 = [m.sb(f"cols_1{p}", [P, N, C], F16) for p in range(2)]
        x_in = [m.sb(f"x_in{i}", [P, W2, C]) for i in range(X_SLOTS)]
        turned = [m.sb(f"x_turned{i}", [P, 2, UW // 2, P], F16) for i in range(2)]
        relu = [m.sb(f"relu{i}", [P, UW, C]) for i in range(2)]
        y_out = [m.sb(f"y_out{i}", [P, W2, C]) for i in range(Y_SLOTS)]
        ps_col = [m.ps(f"ps_col{i}", [P, 2, N]) for i in range(2)]
        ps_turn = [m.ps(f"ps_xt{i}", [P, UW // 2, P]) for i in range(2)]
        ps_y = [m.ps(f"ps_y{i}", [P, UW, C]) for i in range(2)]
        ps_wave = [m.ps(f"ps_wave{i}", [P, UW, C]) for i in range(2)]

        plane_landed = [m.sem(f"d_landed{i}") for i in range(2)]
        plane_high = m.sem("plane_high")
        plane_split = m.sem("plane_split")
        planes_used = m.sem("planes_used")
        col_ready = m.sem("col_ready")
        col_high = m.sem("col_high")
        col_taken = m.sem("col_taken")
        x_landed = [m.sem(f"x_landed{i}") for i in range(X_SLOTS)]
        turn_ready = m.sem("x_turn_ready")
        turn_high = m.sem("x_turn_high")
        turn_low = m.sem("x_turn_low")
        wave_ready = m.sem("wave_ready")
        relu_ready = m.sem("relu_ready")
        y_ready = m.sem("y_ready")
        y_done = m.sem("y_done")
        y_stored = [m.sem(f"y_stored{i}") for i in range(Y_SLOTS)]
        block = m.stack.enter_context(nc.Block())

        U = CHUNKS * UNITS
        PAIRS = C // 2

        def chunk_at(ch):
            return ch // HALVES, ch % HALVES

        @block.sync
        def _(sp):
            def load_planes(b, n):
                sp.wait_ge(plane_split, DC * b + n + 1)
                for q in range(4):
                    g = q % 2
                    if n < D1:
                        K, src, r0 = K1, planes_1, n * D_ROWS
                    else:
                        K, src, r0 = K0, planes_0, (n - D1) * D_ROWS
                    v = src[bass.ds(b, 1), g:g + 2, :, :, :].rearrange("o p k y c -> y (o p k) c")
                    sp.dma_start(stage[n % 2][q * K:(q + 1) * K, :, :], v[:, r0:r0 + D_ROWS, :],
                                 ).then_inc(plane_landed[n % 2], 16)

            def load(b, ch):
                wq, hh = chunk_at(ch)
                sp.wait_ge(turn_ready, b * U + (ch + 1) * UNITS)
                sp.dma_start(x_in[ch % X_SLOTS][:, :, :],
                             x[bass.ds(b, 1), hh * P:(hh + 1) * P, wq * W2:(wq + 1) * W2, :]
                             .rearrange("o h w c -> h (o w) c")).then_inc(x_landed[ch % X_SLOTS], 16)

            def image(b, last):
                for ch in range(CHUNKS):
                    wq, hh = chunk_at(ch)
                    sp.wait_ge(y_done, b * U + (ch + 1) * UNITS + 2)
                    sp.dma_start(y[bass.ds(b, 1), hh * P:(hh + 1) * P, wq * W2:(wq + 1) * W2, :]
                                 .rearrange("o h w c -> h (o w) c"),
                                 y_out[ch % Y_SLOTS][:, :, :]).then_inc(y_stored[ch % Y_SLOTS], 16)
                    if ch + X_SLOTS < CHUNKS:
                        load(b, ch + X_SLOTS)
                    elif not last:
                        load(b + 1, ch + X_SLOTS - CHUNKS)
                    if not last and 3 <= ch < 3 + DC:
                        load_planes(b + 1, ch - 3)

            for i in range(Y_SLOTS):
                sp.sem_inc(y_stored[i], 1)
            for n in range(X_SLOTS):
                load(0, n)
            for n in range(DC):
                load_planes(0, n)
            with sp.Fori(0, B - 1) as b:
                image(b, False)
            image(B - 1, True)
            for i in range(Y_SLOTS):
                sp.wait_ge(y_stored[i], 16 * B * CHUNKS // Y_SLOTS + 1)

        def plane_parts(n):
            rows = 4 * (K1 if n < D1 else K0)
            r0 = (n if n < D1 else n - D1) * D_ROWS
            if n < D1:
                return stage[n % 2][:, :, :], D[1][:, r0:r0 + D_ROWS, :], rows
            src = stage[n % 2][0:rows, :, :].rearrange("p r c -> p (r c)").unsqueeze(1).broadcast_to([rows, 4, D_ROWS * C])
            return src, D[0][:, :, r0:r0 + D_ROWS, :].rearrange("p a r c -> p a (r c)"), rows

        def col_slot(i):
            c0 = 2 * (i % PAIRS)
            if i < PAIRS:
                v = cols_0[:, :, c0:c0 + 2].rearrange("p w c -> p c w")
                return v, v[C:2 * C]
            return [t[:, :, c0:c0 + 2].rearrange("p w c -> p c w") for t in cols_1]

        @block.scalar
        def _(act):
            def plane(b, n):
                act.wait_ge(plane_landed[n % 2], 64 * (b * (DC // 2) + n // 2 + 1))
                if n == 0:
                    act.wait_ge(planes_used, b + 1)
                src, dst, _ = plane_parts(n)
                nc.scalar.activation(dst, src, ACT.Copy).then_inc(plane_high, 1)

            def turn(b, u):
                act.wait_ge(turn_ready, b * U + u + 1 + UNITS * X_SLOTS)
                act.wait_ge(y_ready, b * U + u + 1)
                nc.scalar.activation(turned[u % 2][:, 0, :, :], ps_turn[u % 2][:, :, :], ACT.Copy).then_inc(turn_high, 1)

            def image(b, last):
                turn(b, 0)
                for i in range(2 * PAIRS):
                    act.wait_ge(col_ready, b * 2 * PAIRS + i + 1)
                    nc.scalar.activation(col_slot(i)[0], ps_col[i % 2][:, :, :], ACT.Copy,
                                         scale=1 / 16).then_inc(col_high, 1)
                for u in range(U):
                    act.wait_ge(wave_ready, b * U + u + 1)
                    act.wait_ge(y_done, b * U + u + 1)
                    nc.scalar.activation(relu[u % 2][:, :, :], ps_wave[u % 2][:, :, :], ACT.Relu,
                                         scale=1 / 16).then_inc(relu_ready, 1)
                    if u + 1 < U:
                        turn(b, u + 1)
                    if not last and u % UNITS == 3 and 4 <= u // UNITS < 4 + DC:
                        plane(b + 1, u // UNITS - 4)

            act.sem_inc(relu_ready, 2)
            for n in range(DC):
                plane(0, n)
            with act.Fori(0, B - 1) as b:
                image(b, False)
            image(B - 1, True)

        @block.vector
        def _(dve):
            dve.sem_inc(plane_split, 2)
            dve.sem_inc(col_taken, 2)
            dve.sem_inc(turn_low, 2)
            dve.sem_inc(y_done, 2)

            def plane(b, n):
                dve.wait_ge(plane_high, DC * b + n + 1)
                src, dst, rows = plane_parts(n)
                half = slice(rows // 2, rows)
                nc.vector.tensor_tensor(dst[half], src[half], dst[half], ALU.subtract).then_inc(plane_split, 1)

            def turn(b, u):
                dve.wait_ge(turn_high, b * U + u + 1)
                t = turned[u % 2]
                nc.vector.tensor_tensor(t[:, 1, :, :], ps_turn[u % 2][:, :, :], t[:, 0, :, :],
                                        ALU.subtract).then_inc(turn_low, 1)

            def image(b, last):
                turn(b, 0)
                for i in range(2 * PAIRS):
                    dve.wait_ge(col_high, b * 2 * PAIRS + i + 1)
                    hi, lo = col_slot(i)
                    if i < PAIRS:
                        nc.vector.scalar_tensor_tensor(out=lo, in0=ps_col[i % 2][C:2 * C, :, :], scalar=1 / 16, in1=lo,
                                                       op0=ALU.mult, op1=ALU.subtract).then_inc(col_taken, 1)
                    else:
                        nc.vector.scalar_tensor_tensor(out=lo, in0=ps_col[i % 2][:, :, :], scalar=1 / 16, in1=hi,
                                                       op0=ALU.mult, op1=ALU.subtract).then_inc(col_taken, 1)
                for u in range(U):
                    if u + 1 < U:
                        turn(b, u + 1)
                    ch, j = divmod(u, UNITS)
                    if j == 0:
                        dve.wait_ge(y_stored[ch % Y_SLOTS], b * (16 * CHUNKS // Y_SLOTS) + 16 * (ch // Y_SLOTS) + 1)
                    dve.wait_ge(relu_ready, b * U + u + 3)
                    dve.wait_ge(y_ready, b * U + u + 3)
                    nc.vector.scalar_tensor_tensor(out=y_out[ch % Y_SLOTS][:, j * UW:(j + 1) * UW, :]
                                                   .rearrange("p w c -> p (w c)"),
                                                   in0=ps_y[u % 2][:, :, :].rearrange("p w c -> p (w c)"), scalar=1 / 16,
                                                   in1=relu[u % 2][:, :, :].rearrange("p w c -> p (w c)"),
                                                   op0=ALU.mult, op1=ALU.add).then_inc(y_done, 1)
                    if not last and j == 3 and 4 <= ch < 4 + DC:
                        plane(b + 1, ch - 4)

            for n in range(DC):
                plane(0, n)
            with dve.Fori(0, B - 1) as b:
                image(b, False)
            image(B - 1, True)

        @block.tensor
        def _(pe):
            pe.sem_inc(planes_used, 1)
            pe.sem_inc(turn_ready, UNITS * X_SLOTS)
            pe.sem_inc(y_ready, 2)

            def turn(b, u):
                ch, j = divmod(u, UNITS)
                if j == 0:
                    pe.wait_ge(x_landed[ch % X_SLOTS], 16 * (b * (CHUNKS // X_SLOTS) + ch // X_SLOTS + 1))
                pe.wait_ge(turn_low, b * U + u + 1)
                for k in range(UW // 2):
                    w0 = j * UW + 2 * k
                    last = nc.tensor.transpose(ps_turn[u % 2][:, k, :],
                                               x_in[ch % X_SLOTS][:, w0:w0 + 2, :].rearrange("h w c -> h (w c)"),
                                               w["eye"][:, :])
                last.then_inc(turn_ready, 1)

            with pe.Fori(0, B) as b:
                turn(b, 0)
                pe.wait_ge(plane_split, DC * (b + 1) + 2)
                for i in range(2 * PAIRS):
                    pe.wait_ge(col_taken, b * 2 * PAIRS + i + 1)
                    for j in range(2):
                        c = 2 * (i % PAIRS) + j
                        for q in range(2):
                            if i < PAIRS:
                                lhsT = D[0][:, :, :, c].rearrange("p a r -> p (a r)")
                                rhs = w["waves_w0"][:, q, :]
                            else:
                                lhsT, rhs = D[1][:, :, c], w["waves_w1"][:, q, :]
                            last = nc.tensor.matmul(ps_col[i % 2][:, j, :], lhsT, rhs, start=(q == 0), stop=(q == 1))
                    last.then_inc(col_ready, 1)
                pe.sem_inc(planes_used, 1)
                pe.wait_ge(col_taken, (b + 1) * 2 * PAIRS + 2)
                for u in range(U):
                    ch, j = divmod(u, UNITS)
                    wq, hh = chunk_at(ch)
                    w0 = wq * W2 + j * UW
                    pe.wait_ge(y_done, b * U + u + 1)
                    nc.tensor.matmul(ps_y[u % 2][:, :, :], w["waves_h0"][:, hh, :], cols_0[:, w0:w0 + UW, :],
                                     start=True, stop=False)
                    pe.wait_ge(relu_ready, b * U + u + 1)
                    for n, (p, q) in enumerate(((0, 0), (0, 1), (1, 0))):
                        last = nc.tensor.matmul(ps_wave[u % 2][:, :, :], w["waves_h1"][:, hh, q, :],
                                                cols_1[p][:, w0:w0 + UW, :], start=(n == 0), stop=(n == 2))
                    last.then_inc(wave_ready, 1)
                    if u + 1 < U:
                        turn(b, u + 1)
                    pe.wait_ge(turn_low, b * U + u + 3)
                    for k in range(UW // 2):
                        for n, (p, q) in enumerate(((0, 0), (0, 1), (1, 0))):
                            last = nc.tensor.matmul(
                                ps_y[u % 2][:, 2 * k:2 * k + 2, :].rearrange("h w c -> h (w c)"),
                                turned[u % 2][:, p, k, :],
                                apply[:, bass.ds(b, 1), q, :].rearrange("p o c -> p (o c)"),
                                start=False, stop=(n == 2 and k == UW // 2 - 1))
                    last.then_inc(y_ready, 1)


def dft_constants():
    def parts(a):
        hi = a.astype(np.float16)
        return np.stack([hi, (a - hi).astype(np.float16)], -2)

    def angle(n, k):
        return 2 * np.pi * ((n[:, None] * k[None, :]) % N) / N

    t = {}
    n = np.arange(N)
    a = angle(n, np.arange(K1))
    cos, sin = np.cos(a), np.sin(a)
    e = np.concatenate([cos, -sin], 1)
    t["rows_dft"] = parts(e.reshape(HALVES, P, 2 * K1).transpose(1, 0, 2))
    e = np.stack([np.concatenate([cos, -sin], 1), np.concatenate([sin, cos], 1)], 1)
    e = e.reshape(HALVES, P, 2, 2 * K1).transpose(1, 0, 2, 3)
    hi = e.astype(np.float16)
    t["cols_dft"] = np.stack([hi, (e - hi).astype(np.float16)], 2)

    for name, K in (("waves_w0", K0), ("waves_w1", K1)):
        a = angle(np.arange(K), n)
        weight = np.where(np.arange(K) > 0, 2.0, 1.0)[:, None]
        e = np.concatenate([weight * np.cos(a), -weight * np.sin(a)], 0)
        t[name] = parts(np.concatenate([e, e], 0))
    a = angle(np.arange(K0), n).reshape(K0, HALVES, P)
    e = parts(np.concatenate([np.cos(a), -np.sin(a)], 0))
    t["waves_h0"] = np.concatenate([e[:, :, 0], e[:, :, 1], e[:, :, 0], e[:, :, 1]], 0)
    a = angle(np.concatenate([np.arange(K1), np.arange(N - K1, N)]), n).reshape(KX, HALVES, P)
    t["waves_h1"] = parts(np.concatenate([np.cos(a), -np.sin(a)], 0))
    eye = np.eye(P, dtype=np.float32)
    t["eye"] = eye
    t["minus_eye"] = -eye[:C, :C]
    t["eye_twice"] = np.concatenate([eye[:C, :C]] * 2, 0)
    t["ones"] = np.ones((P, 1), np.float32)
    c = np.arange(P)
    t["sum_parts"] = ((c[:, None] % C == c[None, :] % C) * np.where(c < C, 1, 2)[:, None]).astype(np.float32)
    t["pair_mean"] = (((c[:, None] // 2) == (c[None, :] % C) // 2) * 0.5).astype(np.float32)
    return t


def prepare(nc, w):
    with Memory(nc) as m:
        done = m.sem("prepared")
        block = m.stack.enter_context(nc.Block())

        @block.vector
        def _(dve):
            nc.vector.memset(w["project"][:, :], 0.0).then_inc(done, 1)
            nc.vector.tensor_scalar(w["bias_n"][:, :], w["bias"][:, :], float(N), None, ALU.mult).then_inc(done, 1)
            dve.wait_ge(done, 2)
            for rows, cols in ((slice(0, C), slice(0, C)), (slice(C, 2 * C), slice(C, 2 * C))):
                nc.vector.tensor_tensor(w["project"][rows, cols], w["W"][rows, :], w["eye"][rows, rows],
                                        ALU.add).then_inc(done, 1)
            dve.wait_ge(done, 4)
            nc.vector.tensor_scalar(w["project"][0:C, 2 * C:3 * C], w["project"][0:C, 0:C], -1.0, None,
                                    ALU.mult).then_inc(done, 1)


def two_fourier_layers(nc, x, conv, skip_kernel, skip_bias, fw1, fw2, W, bias, y, tables):
    B = x.shape[0]
    scratch = {}
    for name, shape in (("modes_x", (B, C, K1, 2, K1)), ("planes_0", (B, 3, K0, K0, C)),
                        ("mixed", (2, B, 2, K1, K1, 2 * C)), ("planes_1", (B, 3, KX, K1, C))):
        scratch[name] = nc.dram_tensor(name, shape, F32, kind="Internal").ap()
    with Memory(nc) as m:
        w = {name: m.sb(f"c_{name}", list(t.shape), t.dtype) for name, t in tables.items()}
        loads = [(w[name][:], tables[name]) for name in tables]
        for name, shape in (("skip", [P, C]), ("W", [P, C]), ("project", [P, 3 * C]), ("skip_bias", [C, 1]),
                            ("bias", [1, C]), ("bias_n", [1, C])):
            w[name] = m.sb(f"w_{name}", shape)
        for d in range(2):
            loads.append((w["skip"][d * C:(d + 1) * C, :], skip_kernel))
            loads.append((w["W"][d * C:(d + 1) * C, :], W))
        loads.append((w["skip_bias"][:, :], skip_bias.unsqueeze(1)))
        loads.append((w["bias"][:, :], bias.unsqueeze(0)))
        w["conv"] = conv
        apply = m.sb("apply", [P, B, 2, P], F16)
        load_constants(nc, loads)
        prepare(nc, w)
        with Memory(nc) as mg:
            gram = mg.sb("gram", [P, B, C])
            pass_1(nc, B, x, scratch["modes_x"], gram, w["rows_dft"], w["cols_dft"])
            with Memory(nc) as mm:
                x1_modes = mm.sb("x1_modes", [P, B, K1, 2, K1])
                norm_0(nc, B, gram, apply, scratch["modes_x"], scratch["planes_0"], x1_modes, w)
                mixing_1(nc, B, x1_modes, (fw1, fw2), scratch["mixed"])
            project_1(nc, B, scratch["mixed"], scratch["planes_1"], w)
        pass_2(nc, B, x, y, apply, scratch["planes_0"], scratch["planes_1"], w)


def kernel(x, L0_conv_conv, L0_conv_skip_kernel, L0_conv_skip_bias, L1_conv_fw1, L1_conv_fw2, L1_conv_W, L1_conv_b):
    import concourse.bacc as bacc
    from concourse.bass_utils import run_bass_kernel_spmd

    nc = bacc.Bacc("TRN2", target_bir_lowering=False, num_devices=1)
    given = {"x": x, "conv": L0_conv_conv, "skip_kernel": L0_conv_skip_kernel, "skip_bias": L0_conv_skip_bias,
             "fw1": L1_conv_fw1, "fw2": L1_conv_fw2, "W": L1_conv_W, "b": L1_conv_b}
    arrays = {}

    def take(name, a, kind="ExternalInput"):
        a = np.ascontiguousarray(a)
        arrays[name] = a
        return nc.dram_tensor(name, a.shape, mybir.dt.from_np(a.dtype), kind=kind).ap()

    args = [take(f"in_{name}", a) for name, a in given.items()]
    tables = {name: take(f"table_{name}", a) for name, a in dft_constants().items()}
    y = nc.dram_tensor("out_y", np.shape(x), F32, kind="ExternalOutput").ap()
    two_fourier_layers(nc, *args, y, tables)
    return run_bass_kernel_spmd(nc, [arrays], core_ids=[0]).results[0]["out_y"]
```

```python
from contextlib import ExitStack

import numpy as np

import concourse.bass as bass
from concourse import mybir

F32 = mybir.dt.float32
F16 = mybir.dt.float16
ALU = mybir.AluOpType
ACT = mybir.ActivationFunctionType
AX = mybir.AxisListType

N = 256
C = 64
P = 128
HALVES = N // P
K0 = 16
K1 = 32
EPS = 1e-5

CW = 16
SLOTS = 4
CPH = HALVES * P // CW
CG = 8
GROUPS = C // CG
ROW_BANKS = 4


class Memory:

    def __init__(self, nc):
        self.nc, self.stack = nc, ExitStack()

    def sb(self, name, shape, dt=F32):
        return self.stack.enter_context(self.nc.sbuf_tensor(name, shape, dt))

    def ps(self, name, shape, dt=F32):
        return self.stack.enter_context(self.nc.psum_tensor(name, shape, dt))

    def sem(self, name):
        return self.stack.enter_context(self.nc.semaphore(name))

    def __enter__(self):
        return self

    def __exit__(self, *e):
        return self.stack.__exit__(*e)


def load_constants(nc, pairs):
    with Memory(nc) as m:
        landed = m.sem("constants_landed")
        with nc.Block() as block:
            @block.sync
            def _(sp):
                for dst, src in pairs:
                    sp.dma_start(dst, src).then_inc(landed, 16)
                sp.wait_ge(landed, 16 * len(pairs))


def pass_1(nc, B, x, modes_x, gram, rows_dft, cols_dft):
    with Memory(nc) as m:
        stage = [m.sb(f"stage{s}", [P, CW, C]) for s in range(SLOTS)]
        parts = [m.sb(f"parts{i}", [P, HALVES, P, 2 * C], F16) for i in range(2)]
        rows = m.sb("rows", [P, HALVES, 2, 2, K1, C], F16)
        modes = m.sb("modes", [P, K1 // 2, 2 * K1])
        row_ps = [m.ps(f"row_ps{i}", [P, CG, 2 * K1]) for i in range(ROW_BANKS)]
        gram_ps = m.ps("gram_ps", [P, 512])
        mode_ps = [m.ps(f"mode_ps{i}", [P, K1 // 4, 2 * K1]) for i in range(2)]

        landed = [m.sem(f"chunk_landed{s}") for s in range(SLOTS)]
        high_done = m.sem("high_done")
        split_done = m.sem("split_done")
        half_used = m.sem("half_used")
        gram_ready = m.sem("gram_ready")
        gram_taken = m.sem("gram_taken")
        rows_ready = m.sem("rows_ready")
        rows_high = m.sem("rows_high")
        rows_taken = m.sem("rows_taken")
        modes_ready = m.sem("modes_ready")
        modes_taken = m.sem("modes_taken")
        modes_stored = m.sem("modes_stored")

        block = m.stack.enter_context(nc.Block())

        @block.sync
        def _(sp):
            with sp.Fori(0, B) as b:
                for wh in range(HALVES):
                    for k in range(CPH):
                        hh, w0 = divmod(k * CW, P)
                        c = wh * CPH + k
                        sp.wait_ge(split_done, b * (2 * CPH) + c + 1)
                        sp.dma_start(
                            stage[c % SLOTS][:, :, :],
                            x[bass.ds(b, 1), hh * P:(hh + 1) * P, wh * P + w0:wh * P + w0 + CW, :]
                            .rearrange("o h w c -> h (o w) c"),
                        ).then_inc(landed[c % SLOTS], 16)

        def chunk_parts(c):
            wh, k = divmod(c, CPH)
            hh, w0 = divmod(k * CW, P)
            t = parts[wh][:, hh, w0:w0 + CW, :]
            return t[:, :, 0:C], t[:, :, C:2 * C]

        def row_slot(wh, g):
            return [rows[:, wh, p, :, :, g * CG:(g + 1) * CG].rearrange("w r k c -> w c (r k)")
                    for p in range(2)]

        @block.scalar
        def _(act):
            def high(b, c):
                if c % CPH == 0:
                    act.wait_ge(half_used, 2 * b + c // CPH + 1)
                act.wait_ge(landed[c % SLOTS], 16 * (b * (2 * CPH // SLOTS) + c // SLOTS + 1))
                nc.scalar.activation(chunk_parts(c)[0], stage[c % SLOTS][:, :, :], ACT.Copy).then_inc(high_done, 1)

            def image(b, last):
                for wh in range(HALVES):
                    for g in range(GROUPS):
                        act.wait_ge(rows_ready, (b * HALVES + wh) * GROUPS + g + 1)
                        nc.scalar.activation(row_slot(wh, g)[0], row_ps[g % ROW_BANKS][:, :, :],
                                             ACT.Copy, scale=1 / 16).then_inc(rows_high, 1)
                        for j in range(CPH // GROUPS):
                            c = (wh + 1) * CPH + g * CPH // GROUPS + j
                            if c < 2 * CPH:
                                high(b, c)
                            elif not last:
                                high(b + 1, c - 2 * CPH)
                act.wait_ge(modes_ready, 2 * b + 1)
                act.wait_ge(modes_stored, 32 * b + 1)
                nc.scalar.activation(modes[:, 0:K1 // 4, :], mode_ps[0][:, :, :], ACT.Copy,
                                     scale=1 / 16).then_inc(modes_taken, 1)
                act.wait_ge(modes_taken, 2 * b + 4)
                for q in range(2):
                    dst = modes_x[b:b + 1] if last else modes_x[bass.ds(b, 1), :, :, :, :]
                    act.dma_start(dst.rearrange("o c (k q) r y -> q c (o k) (r y)", q=2)[q],
                                  modes[q * C:(q + 1) * C, :, :]).then_inc(modes_stored, 16)

            act.sem_inc(modes_stored, 1)
            for c in range(CPH):
                high(0, c)
            with act.Fori(0, B - 1) as b:
                image(b, False)
            image(B - 1, True)
            act.wait_ge(modes_stored, 32 * B + 1)

        @block.vector
        def _(dve):
            dve.sem_inc(split_done, SLOTS)
            dve.sem_inc(gram_taken, 1)
            dve.sem_inc(rows_taken, ROW_BANKS)
            dve.sem_inc(modes_taken, 2)

            def low(b, c):
                dve.wait_ge(high_done, b * (2 * CPH) + c + 1)
                hi, lo = chunk_parts(c)
                nc.vector.tensor_tensor(lo, stage[c % SLOTS][:, :, :], hi, ALU.subtract).then_inc(split_done, 1)

            def image(b, last):
                for wh in range(HALVES):
                    for g in range(GROUPS):
                        n = (b * HALVES + wh) * GROUPS + g + 1
                        dve.wait_ge(rows_high, n)
                        hi, lo = row_slot(wh, g)
                        nc.vector.scalar_tensor_tensor(out=lo, in0=row_ps[g % ROW_BANKS][:, :, :], scalar=1 / 16,
                                                       in1=hi, op0=ALU.mult, op1=ALU.subtract).then_inc(rows_taken, 1)
                        for j in range(CPH // GROUPS):
                            c = (wh + 1) * CPH + g * CPH // GROUPS + j
                            if c < 2 * CPH:
                                low(b, c)
                            elif not last:
                                low(b + 1, c - 2 * CPH)
                        if wh == 1 and g == 0:
                            dve.wait_ge(gram_ready, b + 1)
                            nc.vector.tensor_copy(gram[:, bass.ds(b, 1), :].rearrange("p o c -> p (o c)"),
                                                  gram_ps[:, 0:C]).then_inc(gram_taken, 1)
                dve.wait_ge(modes_ready, 2 * b + 2)
                dve.wait_ge(modes_stored, 32 * b + 1)
                nc.vector.tensor_scalar(modes[:, K1 // 4:, :], mode_ps[1][:, :, :], 1 / 16, None,
                                        ALU.mult).then_inc(modes_taken, 1)

            for c in range(CPH):
                low(0, c)
            with dve.Fori(0, B - 1) as b:
                image(b, False)
            image(B - 1, True)

        @block.tensor
        def _(pe):
            pe.sem_inc(half_used, 2)
            with pe.Fori(0, B) as b:
                for wh in range(HALVES):
                    if wh == 0:
                        pe.wait_ge(gram_taken, b + 1)
                    for k in range(CPH):
                        hh, w0 = divmod(k * CW, P)
                        pe.wait_ge(split_done, b * (2 * CPH) + SLOTS + wh * CPH + k + 1)
                        for w in range(w0, w0 + CW):
                            col = parts[wh][:, hh, w, :]
                            last = nc.tensor.matmul(gram_ps[:, 0:C], col, col[:, 0:C],
                                                    start=(wh == 0 and k == 0 and w == w0),
                                                    stop=(wh == 1 and k == CPH - 1 and w == w0 + CW - 1))
                    if wh == 1:
                        last.then_inc(gram_ready, 1)
                    for g in range(GROUPS):
                        pe.wait_ge(rows_taken, (b * HALVES + wh) * GROUPS + g + 1)
                        for c in range(CG):
                            n = 0
                            for hh in range(HALVES):
                                for p, q in ((0, 0), (0, 1), (1, 0)):
                                    last = nc.tensor.matmul(
                                        row_ps[g % ROW_BANKS][:, c, :], parts[wh][:, hh, :, p * C + g * CG + c],
                                        rows_dft[:, hh, q, :], start=(n == 0), stop=(n == 5))
                                    n += 1
                        last.then_inc(rows_ready, 1)
                    pe.sem_inc(half_used, 1)
                pe.wait_ge(rows_taken, (b + 1) * HALVES * GROUPS + ROW_BANKS)
                for i in range(2):
                    pe.wait_ge(modes_taken, 2 * b + i + 1)
                    for j in range(K1 // 4):
                        kx = 2 * (i * K1 // 4 + j)
                        n = 0
                        for wh in range(HALVES):
                            for ri in range(2):
                                for p, q in ((0, 0), (0, 1), (1, 0)):
                                    last = nc.tensor.matmul(
                                        mode_ps[i][:, j, :], rows[:, wh, p, ri, kx:kx + 2, :],
                                        cols_dft[:, wh, q, ri, :], start=(n == 0), stop=(n == 11))
                                    n += 1
                    last.then_inc(modes_ready, 1)


def norm_0(nc, B, gram, apply, modes_x, planes_d, x1_modes, w):
    MODES = K0 * K0
    MC = 64
    MB = 32
    xm = x1_modes
    with Memory(nc) as m:
        products = m.sb("products", [P, B, C])
        scratch = m.sb("scratch", [P, B, C])
        sums = m.sb("sums", [P, 2, B])
        means = m.sb("means", [P, 2, B])
        var = m.sb("var", [P, B])
        std = m.sb("std", [P, B])
        rstd = m.sb("rstd", [P, B])
        shift = m.sb("shift", [P, B])
        A = m.sb("A", [P, B, C])
        const = m.sb("const", [C, B])
        mixed_in = m.sb("mixed_in", [P, MODES, 2, B])
        weights = [m.sb(f"weights{i}", [P, MC, C]) for i in range(2)]
        S = m.sb("S", [C, B, 2, K0, K0])
        S_weighted = m.sb("S_weighted", [C, B, 2, K0, K0])
        S_real = m.sb("S_real", [C, B, 2, K0, K0])
        cross = m.sb("cross", [C, 2, K0, K0])
        cross_sum = m.sb("cross_sum", [C, B])
        planes = [m.sb(f"planes{i}", [P, 3, C]) for i in range(2)]
        zeros = m.sb("zeros", [ROWS - COS_0, (K1 - K0) * C])

        ps_products = m.ps("ps_products", [P, 512])
        ps_small = m.ps("ps_small", [P, 512])
        ps_mix = [m.ps(f"ps_mix{i}", [P, 512]) for i in range(2)]
        ps_apply = [m.ps(f"ps_apply{i}", [P, 512]) for i in range(2)]
        ps_plane = [m.ps(f"ps_plane{i}", [P, 3, C]) for i in range(2)]

        modes_landed = m.sem("modes_landed")
        weights_landed = [m.sem(f"weights_landed{i}") for i in range(2)]
        products_ready = m.sem("products_ready")
        sums_ready = m.sem("sums_ready")
        means_ready = m.sem("means_ready")
        var_ready = m.sem("var_ready")
        std_ready = m.sem("std_ready")
        shift_ready = m.sem("shift_ready")
        const_ready = m.sem("const_ready")
        A_ready = m.sem("A_ready")
        input_ready = m.sem("input_ready")
        mix_ready = m.sem("mix_ready")
        mix_taken = m.sem("mix_taken")
        S_ready = m.sem("S_ready")
        U_ready = m.sem("U_ready")
        U_taken = m.sem("U_taken")
        GA_ready = m.sem("GA_ready")
        AGA_ready = m.sem("AGA_ready")
        square_ready = m.sem("square_ready")
        plane_ready = m.sem("plane_ready")
        plane_taken = m.sem("plane_taken")
        plane_stored = [m.sem(f"plane_stored{i}") for i in range(2)]
        zeroed = m.sem("plane_zeroed")
        zeros_stored = m.sem("zeros_stored")
        x1_ready = m.sem("x1_ready")
        x1_copied = m.sem("x1_copied")
        chain = m.sem("vector_chain")

        block = m.stack.enter_context(nc.Block())
        BANKS = MODES // MB

        @block.sync
        def _(sp):
            for b in range(B):
                for d in range(2):
                    sp.dma_start(xm[d * C:(d + 1) * C, b, :, :, :], modes_x[b]).then_inc(modes_landed, 16)
            for k in range(MODES // MC):
                if k >= 2:
                    sp.wait_ge(mix_ready, (k - 1) * MC // MB)
                for r in range(2):
                    sp.dma_start(
                        weights[k % 2][r * C:(r + 1) * C, :, :],
                        w["conv"][r].rearrange("x y i o -> i (x y) o")[:, k * MC:(k + 1) * MC, :],
                    ).then_inc(weights_landed[k % 2], 16)
            for n in range(2 * B):
                b, q = divmod(n, 2)
                sp.wait_ge(plane_taken, n + 1)
                x0 = q * K0 // 2
                for g in range(2):
                    sp.dma_start(planes_d[b, g, COS_0 + x0:COS_0 + x0 + K0 // 2, 0:K0, :],
                                 planes[n % 2][:, g, :]).then_inc(plane_stored[n % 2], 16)
                    first = 1 if q == 0 else 0
                    sp.dma_start(planes_d[b, g, SIN_0 + x0 + first - 1:SIN_0 + x0 + K0 // 2 - 1, 0:K0, :],
                                 planes[n % 2][first * K0:, g + 1, :]).then_inc(plane_stored[n % 2], 16)
            for i in range(2):
                sp.wait_ge(plane_stored[i], 64 * B)
            sp.wait_ge(x1_ready, 1)
            sp.dma_start(xm[C:2 * C, :, :, :, :], xm[0:C, :, :, :, :]).then_inc(x1_copied, 16)
            sp.wait_ge(x1_copied, 16)

        @block.gpsimd
        def _(pool):
            nc.gpsimd.memset(zeros[:, :], 0.0).then_inc(zeroed, 1)
            pool.wait_ge(zeroed, 1)
            for b in range(B):
                for g in range(2):
                    pool.dma_start(planes_d[b, g, COS_0:ROWS, K0:K1, :].rearrange("k y c -> k (y c)"),
                                   zeros[:, :]).then_inc(zeros_stored, 16)
            pool.wait_ge(zeros_stored, 16 * 2 * B)

        @block.scalar
        def _(act):
            for n in range(2):
                act.wait_ge(var_ready, n + 1)
                nc.scalar.activation(std[0:P >> n, :], var[0:P >> n, :], ACT.Sqrt).then_inc(std_ready, 1)
                if n == 1:
                    break
                for t in range(4 * B):
                    b, q = divmod(t, 4)
                    act.wait_ge(U_ready, t + 1)
                    nc.scalar.activation(xm[0:C, b, :, :, :].rearrange("c x r y -> c (x r y)")[:, q * 512:(q + 1) * 512],
                                         ps_apply[t % 2][0:C, :], ACT.Copy).then_inc(U_taken, 1)
                for t in range(2 * B):
                    act.wait_ge(plane_ready, t + 1)
                    if t >= 2:
                        act.wait_ge(plane_stored[t % 2], 64 * (t // 2))
                    nc.scalar.activation(planes[t % 2][:, :, :], ps_plane[t % 2][:, :, :],
                                         ACT.Copy).then_inc(plane_taken, 1)

        @block.vector
        def _(dve):
            count = [0]

            def step(ins):
                count[0] += 1
                ins.then_inc(chain, 1)
                dve.wait_ge(chain, count[0])

            def norm(n, rows):
                dve.wait_ge(means_ready, n + 1)
                step(nc.vector.tensor_copy(means[0:rows, :, :].rearrange("p s b -> p (s b)"), ps_small[0:rows, 0:2 * B]))
                step(nc.vector.tensor_tensor(var[0:rows, :], means[0:rows, 0, :], means[0:rows, 0, :], ALU.mult))
                step(nc.vector.tensor_tensor(var[0:rows, :], means[0:rows, 1, :], var[0:rows, :], ALU.subtract))
                nc.vector.tensor_scalar(var[0:rows, :], var[0:rows, :], 0.0, EPS, ALU.max, ALU.add).then_inc(var_ready, 1)
                dve.wait_ge(std_ready, n + 1)
                step(nc.vector.reciprocal(rstd[0:rows, :], std[0:rows, :]))
                step(nc.vector.tensor_tensor(std[0:rows, :], rstd[0:rows, :], rstd[0:rows, :], ALU.mult))
                step(nc.vector.tensor_tensor(std[0:rows, :], std[0:rows, :], var[0:rows, :], ALU.mult))
                step(nc.vector.tensor_scalar(std[0:rows, :], std[0:rows, :], -0.5, 1.5, ALU.mult, ALU.add))
                step(nc.vector.tensor_tensor(rstd[0:rows, :], rstd[0:rows, :], std[0:rows, :], ALU.mult))
                nc.vector.scalar_tensor_tensor(out=shift[0:rows, :], in0=means[0:rows, 0, :], scalar=-1.0,
                                               in1=rstd[0:rows, :], op0=ALU.mult, op1=ALU.mult).then_inc(shift_ready, 1)
                dve.wait_ge(shift_ready, n + 1)

            dve.wait_ge(products_ready, 1)
            step(nc.vector.tensor_copy(products[:, :, :].rearrange("p b c -> p (b c)"), ps_products[:, 0:B * C]))
            for b in range(B):
                ins = nc.vector.tensor_tensor(scratch[:, b, :], products[:, b, :], w["eye_twice"][:, :], ALU.mult)
            step(ins)
            step(nc.vector.tensor_reduce(sums[:, 1, :], scratch[:, :, :], AX.X, ALU.add))
            step(nc.vector.tensor_scalar(sums[:, 1, :], sums[:, 1, :], 1 / N / N, None, ALU.mult))
            dve.wait_ge(modes_landed, 32 * B)
            nc.vector.tensor_scalar(sums[:, 0, :], xm[:, :, 0, 0, 0], 1 / N, None, ALU.mult).then_inc(sums_ready, 1)
            norm(0, P)
            for b in range(B):
                ins = nc.vector.scalar_tensor_tensor(out=A[:, b, :], in0=w["skip"][:, :], scalar=rstd[:, b:b + 1],
                                                     in1=w["eye_twice"][:, :], op0=ALU.mult, op1=ALU.add)
            ins.then_inc(A_ready, 1)
            for b in range(B):
                for d in range(2):
                    rows = slice(d * C, (d + 1) * C)
                    for r in range(2):
                        src = xm[rows, b, 0:K0, r if d == 0 else 1 - r, 0:K0]
                        dst = mixed_in[rows, :, r, b].rearrange("p (x y) -> p x y", x=K0)
                        nc.vector.tensor_scalar(dst, src, rstd[rows, b:b + 1], -1.0 if (d, r) == (1, 0) else 1.0,
                                                ALU.mult, ALU.mult)
            dve.wait_ge(const_ready, 1)
            step(nc.vector.tensor_scalar(const[:, :], ps_small[0:C, 64:64 + B], w["skip_bias"][:, 0:1], float(N),
                                         ALU.add, ALU.mult))
            for d in range(2):
                rows = slice(d * C, (d + 1) * C)
                ins = nc.vector.scalar_tensor_tensor(out=mixed_in[rows, 0, d, :], in0=shift[rows, :], scalar=float(N),
                                                     in1=mixed_in[rows, 0, d, :], op0=ALU.mult, op1=ALU.add)
                step(ins)
            dve.sem_inc(input_ready, 1)
            step(nc.vector.tensor_scalar(apply[:, :, 0, :], A[:, :, :], 16.0, None, ALU.mult))
            for b in range(B):
                nc.vector.scalar_tensor_tensor(out=apply[:, b, 1, :], in0=A[:, b, :], scalar=16.0,
                                               in1=apply[:, b, 0, :], op0=ALU.mult, op1=ALU.subtract)
            dve.wait_ge(GA_ready, 1)
            nc.vector.tensor_tensor(scratch[0:C, :, :].rearrange("p b c -> p (b c)"), ps_products[0:C, 0:B * C],
                                    A[0:C, :, :].rearrange("p b c -> p (b c)"), ALU.mult).then_inc(AGA_ready, 1)
            for t in range(BANKS):
                dve.wait_ge(mix_ready, t + 1)
                v = ps_mix[t % 2][0:C, 0:MB * 2 * B].rearrange("p (k r b) -> p k r b", r=2, b=B)
                for r in range(2):
                    for x0 in range(MB // K0):
                        ins = nc.vector.tensor_copy(S[:, :, r, t * MB // K0 + x0, :],
                                                    v[:, x0 * K0:(x0 + 1) * K0, r, :].rearrange("p k b -> p b k"))
                ins.then_inc(mix_taken, 1)
            dve.wait_ge(mix_taken, BANKS)
            nc.vector.tensor_tensor(S[:, :, 0, 0, 0], S[:, :, 0, 0, 0], const[:, :], ALU.add).then_inc(S_ready, 1)
            dve.wait_ge(S_ready, 1)

            def flat(t):
                return t[:, :, :, :, :].rearrange("p b r x y -> p (b r x y)")
            step(nc.vector.tensor_scalar(flat(S_weighted), flat(S), 2.0, None, ALU.mult))
            step(nc.vector.tensor_copy(S_weighted[:, :, :, :, 0], S[:, :, :, :, 0]))
            step(nc.vector.tensor_scalar(flat(S_real), flat(S_weighted), 0.5, None, ALU.mult))
            nc.vector.tensor_copy(S_real[:, :, 0, 0, 0], S[:, :, 0, 0, 0])
            step(nc.vector.memset(S_real[:, :, 1, 0, 0], 0.0))
            dve.wait_ge(U_taken, 4 * B)
            for b in range(B):
                for r in range(2):
                    step(nc.vector.scalar_tensor_tensor(out=cross[:, r, :, :], in0=xm[0:C, b, 0:K0, r, 0:K0], scalar=2.0,
                                                        in1=S_real[:, b, r, :, :], op0=ALU.mult, op1=ALU.add))
                    nc.vector.tensor_tensor(xm[0:C, b, 0:K0, r, 0:K0], xm[0:C, b, 0:K0, r, 0:K0],
                                            S_real[:, b, r, :, :], ALU.add)
                products_of_modes = cross[:, :, :, :].rearrange("p r x y -> p (r x y)")
                step(nc.vector.tensor_tensor(products_of_modes, products_of_modes,
                                             S_weighted[:, b, :, :, :].rearrange("p r x y -> p (r x y)"), ALU.mult))
                step(nc.vector.tensor_reduce(cross_sum[:, b:b + 1], products_of_modes, AX.X, ALU.add))
            dve.wait_ge(square_ready, 1)
            step(nc.vector.tensor_tensor(cross_sum[:, :], cross_sum[:, :], ps_small[0:C, 128:128 + B], ALU.add))
            nc.vector.tensor_scalar(sums[0:C, 0, :], xm[0:C, :, 0, 0, 0], 1 / N, None, ALU.mult).then_inc(sums_ready, 1)
            nc.vector.tensor_scalar(sums[0:C, 1, :], cross_sum[:, :], 1 / N / N, None, ALU.mult).then_inc(sums_ready, 1)
            norm(1, C)
            for b in range(B):
                v = xm[0:C, b, :, :, :].rearrange("p x r y -> p (x r y)")
                ins = nc.vector.tensor_scalar(v, v, rstd[0:C, b:b + 1], None, ALU.mult)
            step(ins)
            nc.vector.scalar_tensor_tensor(out=xm[0:C, :, 0, 0, 0], in0=shift[0:C, :], scalar=float(N),
                                           in1=xm[0:C, :, 0, 0, 0], op0=ALU.mult, op1=ALU.add).then_inc(x1_ready, 1)

        @block.tensor
        def _(pe):
            nc.tensor.matmul(ps_products[:, 0:B * C], w["sum_parts"][:, :],
                             gram[:, :, :].rearrange("p b c -> p (b c)"), start=True, stop=True).then_inc(products_ready, 1)
            pe.wait_ge(sums_ready, 1)
            nc.tensor.matmul(ps_small[:, 0:2 * B], w["pair_mean"][:, :], sums[:, :, :].rearrange("p s b -> p (s b)"),
                             start=True, stop=True).then_inc(means_ready, 1)
            pe.wait_ge(shift_ready, 1)
            nc.tensor.matmul(ps_small[0:C, 64:64 + B], w["skip"][0:C, :], shift[0:C, :],
                             start=True, stop=True).then_inc(const_ready, 1)
            pe.wait_ge(A_ready, 1)
            for b in range(B):
                last = nc.tensor.matmul(ps_products[0:C, b * C:(b + 1) * C], products[0:C, b, :], A[0:C, b, :],
                                        start=True, stop=True)
            last.then_inc(GA_ready, 1)
            pe.wait_ge(input_ready, 1)
            for t in range(BANKS):
                k = t * MB // MC
                if t * MB % MC == 0:
                    pe.wait_ge(weights_landed[k % 2], 32 * (k // 2 + 1))
                if t >= 2:
                    pe.wait_ge(mix_taken, t - 1)
                for j in range(MB):
                    mode = t * MB + j
                    last = nc.tensor.matmul(ps_mix[t % 2][0:C, j * 2 * B:(j + 1) * 2 * B],
                                            weights[k % 2][:, mode % MC, :],
                                            mixed_in[:, mode, :, :].rearrange("p r b -> p (r b)"),
                                            start=True, stop=True)
                last.then_inc(mix_ready, 1)
            for t in range(4 * B):
                b, q = divmod(t, 4)
                if t >= 2:
                    pe.wait_ge(U_taken, t - 1)
                nc.tensor.matmul(ps_apply[t % 2][0:C, :], A[0:C, b, :],
                                 xm[0:C, b, :, :, :].rearrange("c x r y -> c (x r y)")[:, q * 512:(q + 1) * 512],
                                 start=True, stop=True).then_inc(U_ready, 1)
            pe.wait_ge(AGA_ready, 1)
            for b in range(B):
                last = nc.tensor.matmul(ps_small[0:C, 128 + b:129 + b], scratch[0:C, b, :], w["ones"][0:C, 0:1],
                                        start=True, stop=True)
            last.then_inc(square_ready, 1)
            pe.wait_ge(S_ready, 1)
            for t in range(2 * B):
                b, q = divmod(t, 2)
                if t >= 2:
                    pe.wait_ge(plane_taken, t - 1)
                for plane, (r, eye) in enumerate(((0, "eye"), (1, "eye"), (0, "minus_eye"))):
                    src = S[:, b, r, q * (K0 // 2):(q + 1) * (K0 // 2), :].rearrange("c x y -> c (x y)")
                    last = nc.tensor.matmul(ps_plane[t % 2][:, plane, :], src, w[eye][0:C, 0:C], start=True, stop=True)
                last.then_inc(plane_ready, 1)
            pe.wait_ge(sums_ready, 3)
            nc.tensor.matmul(ps_small[0:C, 0:2 * B], w["pair_mean"][0:C, 0:C], sums[0:C, :, :].rearrange("p s b -> p (s b)"),
                             start=True, stop=True).then_inc(means_ready, 1)


def mixing_1(nc, B, x1_modes, fw, mixed):
    KC = 2
    SL = 2
    MG = K1 // 4
    R = 2 * 2 * B
    with Memory(nc) as m:
        weights = [m.sb(f"fw{i}", [P, C, KC, 2 * K1]) for i in range(SL)]
        blocks = [m.sb(f"blocks{i}", [P, 2, B, 2, K1]) for i in range(2)]
        out = [m.sb(f"mix_out{i}", [P, MG, 2 * C]) for i in range(2)]
        zeros = m.sb("mix_zeros", [2 * B, K1 * 2 * C])
        ps = [[m.ps(f"mix_ps{i}{h}", [P, MG // 2, 2 * C]) for h in range(2)] for i in range(2)]

        landed = [m.sem(f"fw_landed{i}") for i in range(SL)]
        zeroed = m.sem("zeroed")
        zeros_stored = m.sem("mix_zeros_stored")
        placed = m.sem("placed")
        ready = m.sem("mix1_ready")
        taken_low = m.sem("mix1_taken_low")
        taken_high = m.sem("mix1_taken_high")
        stored = [m.sem(f"mix1_stored{i}") for i in range(2)]
        block = m.stack.enter_context(nc.Block())
        TURN = SL * KC

        @block.sync
        def _(sp):
            with sp.Fori(0, K1 // TURN) as t:
                for i in range(SL):
                    at = sp.snap((t * SL + i) * (KC * 2 * K1))
                    sp.wait_ge(ready, t * TURN + (i + 1) * KC)
                    for f in range(2):
                        sp.dma_start(weights[i][f * C:(f + 1) * C, :, :, :].rearrange("i o x y -> i o (x y)"),
                                     fw[f].rearrange("i o x y r -> i o (x y r)")
                                     [:, :, bass.ds(at, KC * 2 * K1)],
                                     ).then_inc(landed[i], 16)

        @block.gpsimd
        def _(pool):
            for i in range(2):
                nc.gpsimd.memset(blocks[i][:, :, :, :, :], 0.0).then_inc(zeroed, 1)
            nc.gpsimd.memset(zeros[:, :], 0.0).then_inc(zeroed, 1)
            pool.wait_ge(zeroed, 3)
            for f, k in ((0, K1), (1, 0)):
                pool.dma_start(mixed[f, :, :, k, :, :].rearrange("b r y w -> (b r) (y w)"),
                               zeros[:, :]).then_inc(zeros_stored, 16)
            with pool.Fori(0, K1 // TURN) as t:
                for i in range(TURN):
                    pool.wait_ge(ready, t * TURN + i + 1 + TURN - 2)
                    for f in range(2):
                        rows = slice(f * C, (f + 1) * C)
                        nc.gpsimd.tensor_copy(blocks[i % 2][rows, f, :, :, :].rearrange("p b r y -> p b (r y)"),
                                              x1_modes[rows, :, bass.ds(t * TURN + i, 1), :, :]
                                              .rearrange("p b o r y -> p b (o r y)")).then_inc(placed, 1)
            pool.wait_ge(zeros_stored, 32)

        @block.tensor
        def _(pe):
            pe.sem_inc(ready, TURN)
            with pe.Fori(0, K1 // TURN) as t:
                for i in range(TURN):
                    if i % KC == 0:
                        pe.wait_ge(landed[i // KC], 32 * (t + 1))
                    pe.wait_ge(placed, 2 * (t * TURN + i + 1))
                    pe.wait_ge(taken_low, t * TURN + i + 1)
                    pe.wait_ge(taken_high, t * TURN + i + 1)
                    for h in range(2):
                        for j in range(4):
                            for g in range(h * MG // 2, (h + 1) * MG // 2):
                                y = MG * j + g
                                last = nc.tensor.matmul(
                                    ps[i % 2][h][32 * j:32 * j + R, g % (MG // 2), :],
                                    blocks[i % 2][:, :, :, :, y].rearrange("p f b r -> p (f b r)"),
                                    weights[i // KC][:, :, i % KC, 2 * y:2 * y + 2],
                                    start=True, stop=True, tile_position=(0, 32 * j))
                    last.then_inc(ready, 1)

        def quadrants():
            return [slice(32 * j, 32 * j + R) for j in range(4)] if R < 32 else [slice(0, P)]

        @block.scalar
        def _(act):
            act.sem_inc(taken_low, 2)
            for i in range(2):
                act.sem_inc(stored[i], 1)
            with act.Fori(0, K1 // TURN) as t:
                for i in range(TURN):
                    x = t * TURN + i
                    act.wait_ge(ready, x + 1 + TURN)
                    act.wait_ge(stored[i % 2], t * (128 * TURN // 2) + 128 * (i // 2) + 1)
                    for rows in quadrants():
                        last = nc.scalar.activation(out[i % 2][rows, 0:MG // 2, :], ps[i % 2][0][rows, :, :], ACT.Copy)
                    last.then_inc(taken_low, 1)
                    act.wait_ge(taken_low, x + 3)
                    act.wait_ge(taken_high, x + 3)
                    for f in range(2):
                        k = x if f == 0 else K1 - x
                        for j in range(4):
                            act.dma_start(
                                mixed[f].rearrange("b r k y w -> (b r) k (y w)")
                                [:, bass.ds(k, 1), j * MG * 2 * C:(j + 1) * MG * 2 * C].rearrange("p o w -> p (o w)"),
                                out[i % 2][32 * j + f * R // 2:32 * j + (f + 1) * R // 2, :, :]
                                .rearrange("p g w -> p (g w)")).then_inc(stored[i % 2], 16)
            for i in range(2):
                act.wait_ge(stored[i], 128 * (K1 // 2) + 1)

        @block.vector
        def _(dve):
            dve.sem_inc(taken_high, 2)
            with dve.Fori(0, K1 // TURN) as t:
                for i in range(TURN):
                    x = t * TURN + i
                    dve.wait_ge(ready, x + 1 + TURN)
                    dve.wait_ge(stored[i % 2], t * (128 * TURN // 2) + 128 * (i // 2) + 1)
                    for rows in quadrants():
                        last = nc.vector.tensor_copy(out[i % 2][rows, MG // 2:, :], ps[i % 2][1][rows, :, :])
                    last.then_inc(taken_high, 1)


def project_1(nc, B, mixed, planes_d, w):
    Q = K1 // 4 + 1
    STEP = 3
    STEPS = 2 * Q // STEP
    SCALE = 1.0 / (N * float(np.sqrt(np.float32(N * (N // 2 + 1)))))
    with Memory(nc) as m:
        raw = [m.sb(f"raw{i}", [P, 2, 2, Q, C, 2]) for i in range(2)]
        T = [m.sb(f"T{f}", [P, Q, 2, C]) for f in range(2)]
        GH = m.sb("GH", [P, Q, 2, 2, C])
        turned = [m.sb(f"turned{i}", [P, STEP, P]) for i in range(2)]
        out = [m.sb(f"project_out{i}", [P, Q, 2, 2, C]) for i in range(2)]
        ps_turn = [m.ps(f"ps_turn{i}", [P, STEP, P]) for i in range(2)]
        ps_out = [m.ps(f"ps_out{i}", [P, STEP, 2, C]) for i in range(4)]

        cleared = m.sem("raw_cleared")
        landed = [m.sem(f"raw_landed{i}") for i in range(2)]
        combined = m.sem("combined")
        summed = m.sem("summed")
        turn_ready = m.sem("turn_ready")
        turn_taken = m.sem("turn_taken")
        out_ready = m.sem("out_ready")
        out_taken = m.sem("out_taken")
        biased = m.sem("biased")
        stored = [m.sem(f"planes_stored{i}") for i in range(2)]
        block = m.stack.enter_context(nc.Block())

        @block.sync
        def _(sp):
            for b in range(B):
                if b < 2:
                    sp.wait_ge(cleared, b + 1)
                else:
                    sp.wait_ge(combined, 4 * (b - 1))
                for f in range(2):
                    for r in range(2):
                        src = mixed[f, b, r]
                        sp.dma_start(
                            raw[b % 2][:, f, r, 0:Q - 1, :, :].rearrange("p k o w -> p k (o w)"),
                            src[0:K1].rearrange("(k x) y w -> (x y) k w", x=4)).then_inc(landed[b % 2], 16)
                        sp.dma_start(
                            raw[b % 2][0:K1, f, r, Q - 1, :, :].rearrange("p o w -> p (o w)"),
                            src[K1]).then_inc(landed[b % 2], 16)

        @block.vector
        def _(dve):
            for i in range(2):
                nc.vector.memset(raw[i][:, :, :, Q - 1, :, :].rearrange("p f r o w -> p (f r) (o w)"),
                                 0.0).then_inc(cleared, 1)
            dve.wait_ge(cleared, 2)
            for b in range(B):
                dve.wait_ge(landed[b % 2], 128 * (b // 2 + 1))
                v = raw[b % 2]
                for f in range(2):
                    if b >= 1:
                        dve.wait_ge(summed, 2 * b)
                    nc.vector.tensor_tensor(T[f][:, :, 0, :], v[:, f, 0, :, :, 0], v[:, f, 1, :, :, 1],
                                            ALU.subtract).then_inc(combined, 1)
                    nc.vector.tensor_tensor(T[f][:, :, 1, :], v[:, f, 0, :, :, 1], v[:, f, 1, :, :, 0],
                                            ALU.add).then_inc(combined, 1)
                dve.wait_ge(combined, 4 * (b + 1))
                if b >= 1:
                    dve.wait_ge(turn_ready, b * STEPS)
                for h, op in enumerate((ALU.add, ALU.subtract)):
                    nc.vector.tensor_tensor(GH[:, :, h, :, :].rearrange("p q r c -> p q (r c)"),
                                            T[0][:, :, :, :].rearrange("p q r c -> p q (r c)"),
                                            T[1][:, :, :, :].rearrange("p q r c -> p q (r c)"), op).then_inc(summed, 1)
                for s in range(STEPS):
                    n = b * STEPS + s
                    dve.wait_ge(turn_ready, n + 1)
                    if n >= 2:
                        dve.wait_ge(out_ready, n - 1)
                    nc.vector.tensor_copy(turned[n % 2][:, :, :], ps_turn[n % 2][:, :, :]).then_inc(turn_taken, 1)
                dve.wait_ge(out_taken, b * STEPS + 1)
                at = out[b % 2][0:1, 0, 0, 0, :]
                nc.vector.tensor_tensor(at, at, w["bias_n"][0:1, :], ALU.add).then_inc(biased, 1)

        @block.tensor
        def _(pe):
            def turn(n):
                b, s = divmod(n, STEPS)
                if s == 0:
                    pe.wait_ge(summed, 2 * (b + 1))
                if n >= 2:
                    pe.wait_ge(turn_taken, n - 1)
                for j in range(STEP):
                    q, h = divmod(s * STEP + j, 2)
                    last = nc.tensor.transpose(ps_turn[n % 2][:, j, :], GH[:, q, h, :, :].rearrange("p r c -> p (r c)"),
                                               w["eye"][:, :])
                last.then_inc(turn_ready, 1)

            turn(0)
            for n in range(B * STEPS):
                if n + 1 < B * STEPS:
                    turn(n + 1)
                pe.wait_ge(turn_taken, n + 1)
                if n >= 4:
                    pe.wait_ge(out_taken, n - 3)
                for j in range(STEP):
                    h = (n % STEPS * STEP + j) % 2
                    last = nc.tensor.matmul(ps_out[n % 4][:, j, :, :].rearrange("p a c -> p (a c)"),
                                            turned[n % 2][:, j, :], w["project"][:, h, :], start=True, stop=True)
                last.then_inc(out_ready, 1)

        @block.scalar
        def _(act):
            for b in range(B):
                if b >= 2:
                    act.wait_ge(stored[b % 2], 160 * (b // 2))
                for s in range(STEPS):
                    n = b * STEPS + s
                    act.wait_ge(out_ready, n + 1)
                    nc.scalar.activation(out[b % 2][:, :, :, :, :].rearrange("p q h g c -> p (q h) (g c)")
                                         [:, s * STEP:(s + 1) * STEP, :],
                                         ps_out[n % 4][:, :, :, :].rearrange("p j g c -> p j (g c)"),
                                         ACT.Copy, scale=SCALE).then_inc(out_taken, 1)

        @block.gpsimd
        def _(pool):
            for b in range(B):
                pool.wait_ge(biased, b + 1)
                pool.wait_ge(out_taken, (b + 1) * STEPS)
                v = out[b % 2]
                for g in range(2):
                    dst = planes_d[b, g]
                    for rows, src in (
                        (dst[0:K1].rearrange("(k x) y c -> (x y) k c", x=4), v[:, 0:Q - 1, 0, g, :]),
                        (dst[K1], v[0:K1, Q - 1, 0, g, :]),
                        (dst[SIN_1:SIN_1 + 3].rearrange("x y c -> (x y) c"), v[K1:P, 0, 1, g, :]),
                        (dst[SIN_1 + 3:SIN_1 + K1 - 1].rearrange("(k x) y c -> (x y) k c", x=4), v[:, 1:Q - 1, 1, g, :]),
                        (dst[SIN_1 + K1 - 1], v[0:K1, Q - 1, 1, g, :]),
                    ):
                        pool.dma_start(rows, src).then_inc(stored[b % 2], 16)
            for i in range(min(B, 2)):
                pool.wait_ge(stored[i], 160 * ((B - i + 1) // 2))


COS_1, SIN_1 = 0, K1 + 1
ROWS_1 = 2 * K1 + 1
COS_0, SIN_0 = ROWS_1, ROWS_1 + K0
ROWS = ROWS_1 + 2 * K0 - 1
AGAIN = ROWS
COLS = ROWS + 2 * K0 - 1
WB = 64
BLOCKS = N // WB
W2 = 32
UW = 8
UNITS = W2 // UW
CHUNKS = HALVES * N // W2
U = CHUNKS * UNITS
UB = U // BLOCKS
X_SLOTS = 4
Y_SLOTS = 2
S_UNITS = 2
S_SLOTS = 4
SPLITS = U // S_UNITS
GC = 8
GROUPS_2 = C // GC
D_ROWS = 16
D_CHUNKS = 8


def pass_2(nc, B, x, y, apply, planes, w):
    with Memory(nc) as m:
        stage = [m.sb(f"plane_stage{i}", [P, D_ROWS, C]) for i in range(2)]
        D = m.sb("plane_parts", [P, COLS, C], F16)
        cols = [[m.sb(f"cols{i}{p}", [COLS, WB, C], F16) for p in range(2)] for i in range(2)]
        x_in = [m.sb(f"x_in{i}", [P, W2, C]) for i in range(X_SLOTS)]
        parts = [m.sb(f"x_parts{i}", [P, S_UNITS * UW, 2 * C], F16) for i in range(S_SLOTS)]
        turned = [m.sb(f"x_turned{i}", [P, UW, P], F16) for i in range(2)]
        relu = [m.sb(f"relu{i}", [P, UW, C]) for i in range(2)]
        y_out = [m.sb(f"y_out{i}", [P, W2, C]) for i in range(Y_SLOTS)]
        ps_col = [m.ps(f"ps_col{i}", [P, GC, WB]) for i in range(2)]
        ps_turn = [m.ps(f"ps_xt{i}", [P, UW, P], F16) for i in range(2)]
        ps_y = [m.ps(f"ps_y{i}", [P, UW, C]) for i in range(2)]
        ps_wave = [m.ps(f"ps_wave{i}", [P, UW, C]) for i in range(2)]

        plane_landed = [m.sem(f"plane_landed{i}") for i in range(2)]
        plane_high = m.sem("plane_high")
        plane_split = m.sem("plane_split")
        planes_used = m.sem("planes_used")
        col_ready = m.sem("col_ready")
        col_high = m.sem("col_high")
        col_taken = m.sem("col_taken")
        x_landed = [m.sem(f"x_landed{i}") for i in range(X_SLOTS)]
        x_high = m.sem("x_high")
        x_split = m.sem("x_split")
        turn_ready = m.sem("x_turn_ready")
        turn_taken = m.sem("x_turn_taken")
        wave_ready = m.sem("wave_ready")
        relu_ready = m.sem("relu_ready")
        y_ready = m.sem("y_ready")
        y_done = m.sem("y_done")
        y_stored = [m.sem(f"y_stored{i}") for i in range(Y_SLOTS)]
        block = m.stack.enter_context(nc.Block())

        SPC = W2 // (S_UNITS * UW)
        AHEAD = 3

        def chunk_at(ch):
            return ch // HALVES, ch % HALVES

        def group_of(u):
            t, v = divmod(u, UB)
            if t < BLOCKS - 2 or t == BLOCKS - 2:
                if v < GROUPS_2:
                    return False, t + 1, v
            elif v >= UB - GROUPS_2:
                return True, 0, v - (UB - GROUPS_2)
            return None

        def plane_of(u):
            n = u - (BLOCKS - 2) * UB - GROUPS_2
            return n if 0 <= n < D_CHUNKS else None

        @block.sync
        def _(sp):
            def load_planes(b, n):
                sp.wait_ge(plane_split, D_CHUNKS * b + n + 1)
                r0 = n * D_ROWS if n * D_ROWS < ROWS else n * D_ROWS - AGAIN + COS_0
                rows = min(D_ROWS, ROWS - r0)
                for part in range(2):
                    for g in range(2):
                        q = part * 2 + g
                        sp.dma_start(stage[n % 2][q * K1:(q + 1) * K1, 0:rows, :],
                                     planes[bass.ds(b, 1), g, r0:r0 + rows, :, :].rearrange("o k y c -> y (o k) c"),
                                     ).then_inc(plane_landed[n % 2], 16)

            def load(b, ch):
                wq, hh = chunk_at(ch)
                sp.wait_ge(x_split, (b * CHUNKS + ch + 1) * SPC)
                sp.dma_start(x_in[ch % X_SLOTS][:, :, :],
                             x[bass.ds(b, 1), hh * P:(hh + 1) * P, wq * W2:(wq + 1) * W2, :]
                             .rearrange("o h w c -> h (o w) c")).then_inc(x_landed[ch % X_SLOTS], 16)

            def image(b, last):
                for ch in range(CHUNKS):
                    wq, hh = chunk_at(ch)
                    if not last:
                        for n in {8: (0, 1), 10: (2, 3, 4, 5), 11: (6, 7)}.get(ch, ()):
                            load_planes(b + 1, n)
                    sp.wait_ge(y_done, b * U + (ch + 1) * UNITS + 2)
                    sp.dma_start(y[bass.ds(b, 1), hh * P:(hh + 1) * P, wq * W2:(wq + 1) * W2, :]
                                 .rearrange("o h w c -> h (o w) c"),
                                 y_out[ch % Y_SLOTS][:, :, :]).then_inc(y_stored[ch % Y_SLOTS], 16)
                    if ch + X_SLOTS < CHUNKS:
                        load(b, ch + X_SLOTS)
                    elif not last:
                        load(b + 1, ch + X_SLOTS - CHUNKS)
            for i in range(Y_SLOTS):
                sp.sem_inc(y_stored[i], 1)
            for n in range(D_CHUNKS):
                load_planes(0, n)
                if n < X_SLOTS:
                    load(0, n)
            with sp.Fori(0, B - 1) as b:
                image(b, False)
            image(B - 1, True)
            for i in range(Y_SLOTS):
                sp.wait_ge(y_stored[i], 16 * B * CHUNKS // Y_SLOTS + 1)

        def plane_slot(n):
            rows = min(D_ROWS, COLS - n * D_ROWS)
            return stage[n % 2][:, 0:rows, :], D[:, n * D_ROWS:n * D_ROWS + rows, :]

        def col_slot(t, g):
            return [v[:, :, g * GC:(g + 1) * GC].rearrange("p w c -> p c w") for v in cols[t % 2]]

        def group_number(b, t, g):
            return (b * BLOCKS + t) * GROUPS_2 + g

        @block.scalar
        def _(act):
            def plane(b, n):
                act.wait_ge(plane_landed[n % 2], 64 * (b * (D_CHUNKS // 2) + n // 2 + 1))
                if n == 0:
                    act.wait_ge(planes_used, b + 1)
                src, dst = plane_slot(n)
                nc.scalar.activation(dst, src, ACT.Copy).then_inc(plane_high, 1)

            def columns(b, t, g):
                n = group_number(b, t, g)
                act.wait_ge(col_ready, n + 1)
                nc.scalar.activation(col_slot(t, g)[0], ps_col[g % 2][0:COLS, :, :], ACT.Copy,
                                     scale=1 / 16).then_inc(col_high, 1)

            def split(b, s):
                ch, j = divmod(s, SPC)
                act.wait_ge(x_landed[ch % X_SLOTS], 16 * (b * (CHUNKS // X_SLOTS) + ch // X_SLOTS + 1))
                act.wait_ge(turn_ready, (b * SPLITS + s + 1) * S_UNITS)
                w0 = j * S_UNITS * UW
                nc.scalar.activation(parts[s % S_SLOTS][:, :, 0:C], x_in[ch % X_SLOTS][:, w0:w0 + S_UNITS * UW, :],
                                     ACT.Copy).then_inc(x_high, 1)

            def image(b, last):
                for u in range(U):
                    if u % S_UNITS == 0:
                        s = u // S_UNITS + AHEAD
                        if s < SPLITS:
                            split(b, s)
                        elif not last:
                            split(b + 1, s - SPLITS)
                    act.wait_ge(wave_ready, b * U + u + 1)
                    act.wait_ge(y_done, b * U + u + 1)
                    nc.scalar.activation(relu[u % 2][:, :, :], ps_wave[u % 2][:, :, :], ACT.Relu,
                                         scale=1 / 16).then_inc(relu_ready, 1)
                    if plane_of(u) is not None and not last:
                        plane(b + 1, plane_of(u))
                    if group_of(u):
                        ahead, t, g = group_of(u)
                        if not ahead:
                            columns(b, t, g)
                        elif not last:
                            columns(b + 1, t, g)

            act.sem_inc(relu_ready, 2)
            for s in range(AHEAD):
                split(0, s)
            for n in range(D_CHUNKS):
                plane(0, n)
            for g in range(GROUPS_2):
                columns(0, 0, g)
            with act.Fori(0, B - 1) as b:
                image(b, False)
            image(B - 1, True)

        @block.gpsimd
        def _(pool):
            pool.sem_inc(x_split, X_SLOTS * SPC)
            with pool.Fori(0, B) as b:
                for s in range(SPLITS):
                    ch, j = divmod(s, SPC)
                    w0 = j * S_UNITS * UW
                    pool.wait_ge(x_high, b * SPLITS + s + 1)
                    p = parts[s % S_SLOTS]
                    nc.gpsimd.tensor_tensor(p[:, :, C:2 * C], x_in[ch % X_SLOTS][:, w0:w0 + S_UNITS * UW, :],
                                            p[:, :, 0:C], ALU.subtract).then_inc(x_split, 1)

        @block.vector
        def _(dve):
            dve.sem_inc(plane_split, 2)
            dve.sem_inc(col_taken, 2)
            dve.sem_inc(turn_taken, 2)
            dve.sem_inc(y_done, 2)

            def plane(b, n):
                dve.wait_ge(plane_high, D_CHUNKS * b + n + 1)
                src, dst = plane_slot(n)
                nc.vector.tensor_tensor(dst[C:P], src[C:P], dst[C:P], ALU.subtract).then_inc(plane_split, 1)

            def columns(b, t, g):
                dve.wait_ge(col_high, group_number(b, t, g) + 1)
                hi, lo = col_slot(t, g)
                nc.vector.scalar_tensor_tensor(out=lo, in0=ps_col[g % 2][0:COLS, :, :], scalar=1 / 16, in1=hi,
                                               op0=ALU.mult, op1=ALU.subtract).then_inc(col_taken, 1)

            def turn(b, u):
                dve.wait_ge(turn_ready, b * U + u + 1 + S_SLOTS * S_UNITS)
                dve.wait_ge(y_ready, b * U + u + 1)
                nc.vector.tensor_scalar(turned[u % 2][:, :, :].rearrange("p w h -> p (w h)").bitcast(mybir.dt.uint32),
                                        ps_turn[u % 2][:, :, :].rearrange("p w h -> p (w h)").bitcast(mybir.dt.uint32),
                                        0, None, ALU.bitwise_or).then_inc(turn_taken, 1)

            def image(b, last):
                for u in range(U):
                    if u + 1 < U:
                        turn(b, u + 1)
                    elif not last:
                        turn(b + 1, 0)
                    ch, j = divmod(u, UNITS)
                    if j == 0:
                        dve.wait_ge(y_stored[ch % Y_SLOTS], b * (16 * CHUNKS // Y_SLOTS) + 16 * (ch // Y_SLOTS) + 1)
                    dve.wait_ge(relu_ready, b * U + u + 3)
                    dve.wait_ge(y_ready, b * U + u + 3)
                    nc.vector.scalar_tensor_tensor(out=y_out[ch % Y_SLOTS][:, j * UW:(j + 1) * UW, :]
                                                   .rearrange("p w c -> p (w c)"),
                                                   in0=ps_y[u % 2][:, :, :].rearrange("p w c -> p (w c)"), scalar=1 / 16,
                                                   in1=relu[u % 2][:, :, :].rearrange("p w c -> p (w c)"),
                                                   op0=ALU.mult, op1=ALU.add).then_inc(y_done, 1)
                    if plane_of(u) is not None and not last:
                        plane(b + 1, plane_of(u))
                    if group_of(u):
                        ahead, t, g = group_of(u)
                        if not ahead:
                            columns(b, t, g)
                        elif not last:
                            columns(b + 1, t, g)

            for n in range(D_CHUNKS):
                plane(0, n)
            for g in range(GROUPS_2):
                columns(0, 0, g)
            turn(0, 0)
            with dve.Fori(0, B - 1) as b:
                image(b, False)
            image(B - 1, True)

        @block.tensor
        def _(pe):
            pe.sem_inc(planes_used, 1)
            pe.sem_inc(turn_ready, S_UNITS * S_SLOTS)
            pe.sem_inc(y_ready, 2)

            def turn(b, u):
                s, j = divmod(u, S_UNITS)
                pe.wait_ge(x_split, b * SPLITS + s + 1 + X_SLOTS * SPC)
                pe.wait_ge(turn_taken, b * U + u + 1)
                for k in range(UW):
                    last = nc.tensor.transpose(ps_turn[u % 2][:, k, :], parts[s % S_SLOTS][:, j * UW + k, :],
                                               w["eye_16"][:, :])
                last.then_inc(turn_ready, 1)

            def columns(b, t, g):
                n = group_number(b, t, g)
                pe.wait_ge(col_taken, n + 1)
                if (t, g) == (0, 0):
                    pe.wait_ge(plane_split, D_CHUNKS * (b + 1) + 2)
                for c in range(GC):
                    for q in range(2):
                        last = nc.tensor.matmul(ps_col[g % 2][0:COLS, c, :], D[:, :, g * GC + c],
                                                w["waves_w"][:, q, t * WB:(t + 1) * WB], start=(q == 0), stop=(q == 1))
                last.then_inc(col_ready, 1)
                if (t, g) == (BLOCKS - 1, GROUPS_2 - 1):
                    pe.sem_inc(planes_used, 1)

            def image(b, last):
                for u in range(U):
                    ch, j = divmod(u, UNITS)
                    wq, hh = chunk_at(ch)
                    t = u // UB
                    w0 = wq * W2 + j * UW - t * WB
                    high, low = (v[:, w0:w0 + UW, :] for v in cols[t % 2])
                    if u % UB == 0:
                        pe.wait_ge(col_taken, group_number(b, t, GROUPS_2 - 1) + 3)
                    pe.wait_ge(relu_ready, b * U + u + 1)
                    for n, (q, v) in enumerate(((0, high), (1, high), (2, low))):
                        mm = nc.tensor.matmul(ps_wave[u % 2][:, :, :], w["waves_h1"][:, hh, q, :], v,
                                              start=(n == 0), stop=(n == 2))
                    mm.then_inc(wave_ready, 1)
                    pe.wait_ge(y_done, b * U + u + 1)
                    for n, (q, v) in enumerate(((0, high), (1, low))):
                        nc.tensor.matmul(ps_y[u % 2][:, :, :], w["waves_h0"][:, hh, q, :], v, start=(n == 0), stop=False)
                    if u + 1 < U:
                        turn(b, u + 1)
                    elif not last:
                        turn(b + 1, 0)
                    pe.wait_ge(turn_taken, b * U + u + 3)
                    for k in range(UW):
                        for q in range(2):
                            mm = nc.tensor.matmul(
                                ps_y[u % 2][:, k, :], turned[u % 2][:, k, :],
                                apply[:, bass.ds(b, 1), q, :].rearrange("p o c -> p (o c)"),
                                start=False, stop=(q == 1 and k == UW - 1))
                    mm.then_inc(y_ready, 1)
                    if group_of(u):
                        ahead, tt, g = group_of(u)
                        if not ahead:
                            columns(b, tt, g)
                        elif not last:
                            columns(b + 1, tt, g)

            for g in range(GROUPS_2):
                columns(0, 0, g)
            turn(0, 0)
            with pe.Fori(0, B - 1) as b:
                image(b, False)
            image(B - 1, True)


def dft_constants():
    def parts(a):
        hi = a.astype(np.float16)
        return np.stack([hi, (a - hi).astype(np.float16)], -2)

    def angle(n, k):
        return 2 * np.pi * ((n[:, None] * k[None, :]) % N) / N

    t = {}
    n = np.arange(N)
    a = angle(n, np.arange(K1))
    cos, sin = np.cos(a), np.sin(a)
    e = np.concatenate([cos, -sin], 1)
    t["rows_dft"] = parts(e.reshape(HALVES, P, 2 * K1).transpose(1, 0, 2))
    e = np.stack([np.concatenate([cos, -sin], 1), np.concatenate([sin, cos], 1)], 1)
    e = e.reshape(HALVES, P, 2, 2 * K1).transpose(1, 0, 2, 3)
    hi = e.astype(np.float16)
    t["cols_dft"] = np.stack([hi, (e - hi).astype(np.float16)], 2)

    a = angle(np.arange(K1), n)
    weight = np.where(np.arange(K1) > 0, 2.0, 1.0)[:, None]
    e = np.concatenate([weight * np.cos(a), -weight * np.sin(a)], 0)
    t["waves_w"] = parts(np.concatenate([e, e], 0))
    k = np.arange(K1 + 1)
    a = angle(k, n)
    rows_1, rows_0 = np.zeros((COLS, N)), np.zeros((COLS, N))
    rows_1[COS_1:SIN_1], rows_1[SIN_1:ROWS_1] = np.cos(a), -np.sin(a[1:])
    rows_0[COS_0:SIN_0], rows_0[SIN_0:ROWS] = np.cos(a[:K0]), -np.sin(a[1:K0])
    high_1, low_1 = parts(rows_1.reshape(COLS, HALVES, P)).transpose(2, 0, 1, 3)
    high_0, low_0 = parts(rows_0.reshape(COLS, HALVES, P)).transpose(2, 0, 1, 3)
    t["waves_h1"] = np.stack([high_1, low_1, high_1], 2)
    both = high_0.copy()
    both[AGAIN:] = low_0[COS_0:ROWS]
    t["waves_h0"] = np.stack([both, high_0], 2)
    t["eye_16"] = np.eye(P, dtype=np.float16)
    eye = np.eye(P, dtype=np.float32)
    t["eye"] = eye
    t["minus_eye"] = -eye[:C, :C]
    t["eye_twice"] = np.concatenate([eye[:C, :C]] * 2, 0)
    t["ones"] = np.ones((P, 1), np.float32)
    c = np.arange(P)
    t["sum_parts"] = ((c[:, None] % C == c[None, :] % C) * np.where(c < C, 1, 2)[:, None]).astype(np.float32)
    t["pair_mean"] = (((c[:, None] // 2) == (c[None, :] % C) // 2) * 0.5).astype(np.float32)
    return t


def prepare(nc, w):
    with Memory(nc) as m:
        done = m.sem("prepared")
        block = m.stack.enter_context(nc.Block())

        @block.vector
        def _(dve):
            project, re, im = w["project"], slice(0, C), slice(C, 2 * C)
            nc.vector.memset(project[:, :, :], 0.0).then_inc(done, 1)
            nc.vector.tensor_scalar(w["bias_n"][:, :], w["bias"][:, :], float(N), None, ALU.mult).then_inc(done, 1)
            dve.wait_ge(done, 2)
            for h, rows, cols in ((0, re, re), (0, im, im), (1, im, re)):
                nc.vector.tensor_tensor(project[rows, h, cols], w["W"][rows, :], w["eye"][rows, rows],
                                        ALU.add).then_inc(done, 1)
            dve.wait_ge(done, 5)
            nc.vector.tensor_scalar(project[re, 1, im], project[re, 0, re], -1.0, None, ALU.mult).then_inc(done, 1)


def two_fourier_layers(nc, x, conv, skip_kernel, skip_bias, fw1, fw2, W, bias, y, tables):
    B = x.shape[0]
    scratch = {}
    for name, shape in (("modes_x", (B, C, K1, 2, K1)), ("planes", (B, 2, ROWS, K1, C)),
                        ("mixed", (2, B, 2, K1 + 1, K1, 2 * C))):
        scratch[name] = nc.dram_tensor(name, shape, F32, kind="Internal").ap()
    with Memory(nc) as m:
        w = {name: m.sb(f"c_{name}", list(t.shape), t.dtype) for name, t in tables.items()}
        loads = [(w[name][:], tables[name]) for name in tables]
        for name, shape in (("skip", [P, C]), ("W", [P, C]), ("project", [P, 2, 2 * C]), ("skip_bias", [C, 1]),
                            ("bias", [1, C]), ("bias_n", [1, C])):
            w[name] = m.sb(f"w_{name}", shape)
        for d in range(2):
            loads.append((w["skip"][d * C:(d + 1) * C, :], skip_kernel))
            loads.append((w["W"][d * C:(d + 1) * C, :], W))
        loads.append((w["skip_bias"][:, :], skip_bias.unsqueeze(1)))
        loads.append((w["bias"][:, :], bias.unsqueeze(0)))
        w["conv"] = conv
        apply = m.sb("apply", [P, B, 2, C], F16)
        load_constants(nc, loads)
        prepare(nc, w)
        with Memory(nc) as mg:
            gram = mg.sb("gram", [P, B, C])
            pass_1(nc, B, x, scratch["modes_x"], gram, w["rows_dft"], w["cols_dft"])
            with Memory(nc) as mm:
                x1_modes = mm.sb("x1_modes", [P, B, K1, 2, K1])
                norm_0(nc, B, gram, apply, scratch["modes_x"], scratch["planes"], x1_modes, w)
                mixing_1(nc, B, x1_modes, (fw1, fw2), scratch["mixed"])
            project_1(nc, B, scratch["mixed"], scratch["planes"], w)
        pass_2(nc, B, x, y, apply, scratch["planes"], w)


def kernel(x, L0_conv_conv, L0_conv_skip_kernel, L0_conv_skip_bias, L1_conv_fw1, L1_conv_fw2, L1_conv_W, L1_conv_b):
    import concourse.bacc as bacc
    from concourse.bass_utils import run_bass_kernel_spmd

    nc = bacc.Bacc("TRN2", target_bir_lowering=False, num_devices=1)
    given = {"x": x, "conv": L0_conv_conv, "skip_kernel": L0_conv_skip_kernel, "skip_bias": L0_conv_skip_bias,
             "fw1": L1_conv_fw1, "fw2": L1_conv_fw2, "W": L1_conv_W, "b": L1_conv_b}
    arrays = {}

    def take(name, a, kind="ExternalInput"):
        a = np.ascontiguousarray(a)
        arrays[name] = a
        return nc.dram_tensor(name, a.shape, mybir.dt.from_np(a.dtype), kind=kind).ap()

    args = [take(f"in_{name}", a) for name, a in given.items()]
    tables = {name: take(f"table_{name}", a) for name, a in dft_constants().items()}
    y = nc.dram_tensor("out_y", np.shape(x), F32, kind="ExternalOutput").ap()
    two_fourier_layers(nc, *args, y, tables)
    return run_bass_kernel_spmd(nc, [arrays], core_ids=[0]).results[0]["out_y"]
```

```python
from contextlib import ExitStack

import numpy as np

import concourse.bass as bass
from concourse import mybir

F32 = mybir.dt.float32
F16 = mybir.dt.float16
ALU = mybir.AluOpType
ACT = mybir.ActivationFunctionType
AX = mybir.AxisListType

N = 256
C = 64
P = 128
HALVES = N // P
K0 = 16
K1 = 32
EPS = 1e-5

CW = 16
SLOTS = 8
CPH = HALVES * P // CW
CG = 8
GROUPS = C // CG
ROW_BANKS = 4

KC = 2


class Memory:

    def __init__(self, nc):
        self.nc, self.stack = nc, ExitStack()

    def sb(self, name, shape, dt=F32):
        return self.stack.enter_context(self.nc.sbuf_tensor(name, shape, dt))

    def ps(self, name, shape, dt=F32):
        return self.stack.enter_context(self.nc.psum_tensor(name, shape, dt))

    def sem(self, name):
        return self.stack.enter_context(self.nc.semaphore(name))

    def __enter__(self):
        return self

    def __exit__(self, *e):
        return self.stack.__exit__(*e)


def load_constants(nc, pairs):
    with Memory(nc) as m:
        landed = m.sem("constants_landed")
        with nc.Block() as block:
            @block.sync
            def _(sp):
                for dst, src in pairs:
                    sp.dma_start(dst, src).then_inc(landed, 16)
                sp.wait_ge(landed, 16 * len(pairs))


def pass_1(nc, B, x, modes_x, gram, rows_dft, cols_dft):
    with Memory(nc) as m:
        stage = [m.sb(f"stage{s}", [P, CW, C]) for s in range(SLOTS)]
        parts = [m.sb(f"parts{i}", [P, HALVES, P, 2 * C], F16) for i in range(2)]
        rows = m.sb("rows", [P, HALVES, 2, 2, K1, C], F16)
        modes = m.sb("modes", [P, K1 // 2, 2 * K1])
        row_ps = [m.ps(f"row_ps{i}", [P, CG, 2 * K1]) for i in range(ROW_BANKS)]
        gram_ps = m.ps("gram_ps", [P, 512])
        mode_ps = [m.ps(f"mode_ps{i}", [P, K1 // 4, 2 * K1]) for i in range(2)]

        landed = [m.sem(f"chunk_landed{s}") for s in range(SLOTS)]
        high_act = m.sem("high_act")
        high_dve = m.sem("high_dve")
        low = [m.sem("low_dve"), m.sem("low_pool")]
        half_used = m.sem("half_used")
        gram_ready = m.sem("gram_ready")
        gram_taken = m.sem("gram_taken")
        rows_ready = m.sem("rows_ready")
        rows_high = m.sem("rows_high")
        rows_taken = m.sem("rows_taken")
        modes_ready = m.sem("modes_ready")
        modes_taken = m.sem("modes_taken")
        modes_stored = m.sem("modes_stored")

        block = m.stack.enter_context(nc.Block())
        IC = 2 * CPH
        SPLITS_BESIDE = (3, 3, 3, 3, 2, 2, 0, 0)
        CPG = CPH // GROUPS
        LAG = 2 * CPG

        def low_count(b, c):
            return b * (IC // 2) + c // 2 + 1

        @block.sync
        def _(sp):
            with sp.Fori(0, B) as b:
                for c in range(IC):
                    wh, k = divmod(c, CPH)
                    hh, w0 = divmod(k * CW, P)
                    sp.wait_ge(low[c % 2], low_count(b, c))
                    sp.dma_start(
                        stage[c % SLOTS][:, :, :],
                        x[bass.ds(b, 1), hh * P:(hh + 1) * P, wh * P + w0:wh * P + w0 + CW, :]
                        .rearrange("o h w c -> h (o w) c"),
                    ).then_inc(landed[c % SLOTS], 16)

        def chunk_parts(c):
            wh, k = divmod(c, CPH)
            hh, w0 = divmod(k * CW, P)
            t = parts[wh][:, hh, w0:w0 + CW, :]
            return t[:, :, 0:C], t[:, :, C:2 * C]

        def beside(b, wh, g, last, multiply=False):
            if multiply:
                first, count = g * CPG - LAG, CPG
            else:
                first, count = sum(SPLITS_BESIDE[:g]), SPLITS_BESIDE[g]
            for c in range((wh + 1) * CPH + first, (wh + 1) * CPH + first + count):
                if c < IC:
                    yield b, c
                elif not last:
                    yield b + 1, c - IC

        def row_slot(wh, g):
            return [rows[:, wh, p, :, :, g * CG:(g + 1) * CG].rearrange("w r k c -> w c (r k)")
                    for p in range(2)]

        def wait_for_chunk(eng, b, c):
            eng.wait_ge(landed[c % SLOTS], 16 * (b * (IC // SLOTS) + c // SLOTS + 1))
            if c % CPH < 2:
                eng.wait_ge(half_used, 2 * b + c // CPH + 1)

        @block.scalar
        def _(act):
            def split(b, c):
                if c % 4:
                    wait_for_chunk(act, b, c)
                    nc.scalar.activation(chunk_parts(c)[0], stage[c % SLOTS][:, :, :], ACT.Copy).then_inc(high_act, 1)

            def image(b, last):
                for wh in range(HALVES):
                    for g in range(GROUPS):
                        act.wait_ge(rows_ready, (b * HALVES + wh) * GROUPS + g + 1)
                        nc.scalar.activation(row_slot(wh, g)[0], row_ps[g % ROW_BANKS][:, :, :],
                                             ACT.Copy, scale=1 / 16).then_inc(rows_high, 1)
                        for at in beside(b, wh, g, last):
                            split(*at)
                act.wait_ge(modes_ready, 2 * b + 1)
                act.wait_ge(modes_stored, 32 * b + 1)
                nc.scalar.activation(modes[:, 0:K1 // 4, :], mode_ps[0][:, :, :], ACT.Copy,
                                     scale=1 / 16).then_inc(modes_taken, 1)
                act.wait_ge(modes_taken, 2 * b + 4)
                for q in range(2):
                    dst = modes_x[b:b + 1] if last else modes_x[bass.ds(b, 1), :, :, :, :]
                    act.dma_start(dst.rearrange("o c (k q) r y -> q c (o k) (r y)", q=2)[q],
                                  modes[q * C:(q + 1) * C, :, :]).then_inc(modes_stored, 16)

            act.sem_inc(modes_stored, 1)
            for c in range(CPH):
                split(0, c)
            with act.Fori(0, B - 1) as b:
                image(b, False)
            image(B - 1, True)
            act.wait_ge(modes_stored, 32 * B + 1)

        def wait_for_high(eng, b, c):
            if c % 4 == 0:
                eng.wait_ge(high_dve, b * (IC // 4) + c // 4 + 1)
            else:
                eng.wait_ge(high_act, b * (IC * 3 // 4) + c - c // 4)

        @block.gpsimd
        def _(pool):
            pool.sem_inc(low[1], SLOTS // 2)
            with pool.Fori(0, B) as b:
                for c in range(1, IC, 2):
                    wait_for_high(pool, b, c)
                    hi, lo = chunk_parts(c)
                    nc.gpsimd.tensor_tensor(lo, stage[c % SLOTS][:, :, :], hi, ALU.subtract).then_inc(low[1], 1)

        @block.vector
        def _(dve):
            dve.sem_inc(low[0], SLOTS // 2)
            dve.sem_inc(gram_taken, 1)
            dve.sem_inc(rows_taken, ROW_BANKS)
            dve.sem_inc(modes_taken, 2)

            def split(b, c):
                hi, lo = chunk_parts(c)
                if c % 4 == 0:
                    wait_for_chunk(dve, b, c)
                    nc.vector.tensor_copy(hi, stage[c % SLOTS][:, :, :]).then_inc(high_dve, 1)
                if c % 2 == 0:
                    wait_for_high(dve, b, c)
                    nc.vector.tensor_tensor(lo, stage[c % SLOTS][:, :, :], hi, ALU.subtract).then_inc(low[0], 1)

            def image(b, last):
                for wh in range(HALVES):
                    for g in range(GROUPS):
                        dve.wait_ge(rows_high, (b * HALVES + wh) * GROUPS + g + 1)
                        hi, lo = row_slot(wh, g)
                        nc.vector.scalar_tensor_tensor(out=lo, in0=row_ps[g % ROW_BANKS][:, :, :], scalar=1 / 16,
                                                       in1=hi, op0=ALU.mult, op1=ALU.subtract).then_inc(rows_taken, 1)
                        if wh == 1 and g == LAG // CPG:
                            dve.wait_ge(gram_ready, b + 1)
                            nc.vector.tensor_copy(gram[:, bass.ds(b, 1), :].rearrange("p o c -> p (o c)"),
                                                  gram_ps[:, 0:C]).then_inc(gram_taken, 1)
                        for at in beside(b, wh, g, last):
                            split(*at)
                dve.wait_ge(modes_ready, 2 * b + 2)
                dve.wait_ge(modes_stored, 32 * b + 1)
                nc.vector.tensor_scalar(modes[:, K1 // 4:, :], mode_ps[1][:, :, :], 1 / 16, None,
                                        ALU.mult).then_inc(modes_taken, 1)

            for c in range(CPH):
                split(0, c)
            with dve.Fori(0, B - 1) as b:
                image(b, False)
            image(B - 1, True)

        @block.tensor
        def _(pe):
            def products(b, c):
                wh, k = divmod(c, CPH)
                hh, w0 = divmod(k * CW, P)
                if c == 0:
                    pe.wait_ge(gram_taken, b + 1)
                pe.wait_ge(low[c % 2], low_count(b, c) + SLOTS // 2)
                for w in range(w0, w0 + CW):
                    col = parts[wh][:, hh, w, :]
                    last = nc.tensor.matmul(gram_ps[:, 0:C], col, col[:, 0:C], start=(c == 0 and w == w0),
                                            stop=(c == IC - 1 and w == w0 + CW - 1))
                if c == IC - 1:
                    last.then_inc(gram_ready, 1)

            def image(b, last_image):
                for wh in range(HALVES):
                    for i in range(2):
                        pe.wait_ge(low[i], low_count(b, (wh + 1) * CPH - 1) + SLOTS // 2)
                    for g in range(GROUPS):
                        pe.wait_ge(rows_taken, (b * HALVES + wh) * GROUPS + g + 1)
                        for c in range(CG):
                            n = 0
                            for hh in range(HALVES):
                                for p, q in ((0, 0), (0, 1), (1, 0)):
                                    last = nc.tensor.matmul(
                                        row_ps[g % ROW_BANKS][:, c, :], parts[wh][:, hh, :, p * C + g * CG + c],
                                        rows_dft[:, hh, q, :], start=(n == 0), stop=(n == 5))
                                    n += 1
                        last.then_inc(rows_ready, 1)
                        if g == GROUPS - 1 and wh == 0:
                            pe.sem_inc(half_used, 1)
                        for at in beside(b, wh, g, last_image, multiply=True):
                            products(*at)
                    if wh == 1:
                        pe.sem_inc(half_used, 1)
                pe.wait_ge(rows_taken, (b + 1) * HALVES * GROUPS + ROW_BANKS)
                for i in range(2):
                    pe.wait_ge(modes_taken, 2 * b + i + 1)
                    for j in range(K1 // 4):
                        kx = 2 * (i * K1 // 4 + j)
                        n = 0
                        for wh in range(HALVES):
                            for ri in range(2):
                                for p, q in ((0, 0), (0, 1), (1, 0)):
                                    last = nc.tensor.matmul(
                                        mode_ps[i][:, j, :], rows[:, wh, p, ri, kx:kx + 2, :],
                                        cols_dft[:, wh, q, ri, :], start=(n == 0), stop=(n == 11))
                                    n += 1
                    last.then_inc(modes_ready, 1)

            pe.sem_inc(half_used, 2)
            for c in range(CPH - LAG):
                products(0, c)
            with pe.Fori(0, B - 1) as b:
                image(b, False)
            image(B - 1, True)


def fw_slot(weights, f):
    return weights[f * C:(f + 1) * C, :, :, :].rearrange("i o x y -> i o (x y)")


def fw_chunk(fw, at):
    return fw.rearrange("i o x y r -> i o (x y r)")[:, :, bass.ds(at, KC * 2 * K1)]


def norm_0(nc, B, gram, apply, modes_x, planes_d, x1_modes, fw, fw_first, w):
    MODES = K0 * K0
    MC = 64
    MB = 32
    XB = 8
    xm = x1_modes
    with Memory(nc) as m:
        products = m.sb("products", [P, B, C])
        scratch = m.sb("scratch", [P, B, C])
        sums = m.sb("sums", [P, 2, B])
        means = m.sb("means", [P, 2, B])
        var = m.sb("var", [P, B])
        std = m.sb("std", [P, B])
        rstd = m.sb("rstd", [P, B])
        shift = m.sb("shift", [P, B])
        A = m.sb("A", [P, B, C])
        const = m.sb("const", [C, B])
        mixed_in = m.sb("mixed_in", [P, MODES, 2, B])
        weights = [fw_first[:, :, :, :].rearrange("p o x y -> p (o x y)")[:, i * MC * C:(i + 1) * MC * C]
                   .rearrange("p (m o) -> p m o", o=C) for i in range(2)]
        S = m.sb("S", [C, 2, K0, B, K0])
        S_weighted = m.sb("S_weighted", [C, 2, K0, B, K0])
        S_real = m.sb("S_real", [C, 2, K0, B, K0])
        cross_sum = m.sb("cross_sum", [C, B])
        planes = [m.sb(f"planes{i}", [B * K0, XB, C]) for i in range(2)]
        xm_parts = [m.sb(f"xm_parts{i}", [C, 2, 512], F16) for i in range(2)]
        plane_parts = m.sb("plane_parts", [B * K0, 3, 2, K0, C], F16)
        zeros = m.sb("zeros", [B * (K1 - K0), (ROWS - COS_0) * C], F16)

        ps_products = m.ps("ps_products", [P, 512])
        ps_small = m.ps("ps_small", [P, 512])
        ps_mix = [m.ps(f"ps_mix{i}", [P, 512]) for i in range(2)]
        ps_apply = [m.ps(f"ps_apply{i}", [P, 512]) for i in range(2)]
        ps_plane = [m.ps(f"ps_plane{i}", [P, XB, C]) for i in range(2)]

        modes_landed = m.sem("modes_landed")
        fw_landed = m.sem("fw_first_landed")
        weights_landed = [m.sem(f"weights_landed{i}") for i in range(2)]
        products_ready = m.sem("products_ready")
        sums_ready = m.sem("sums_ready")
        means_ready = m.sem("means_ready")
        var_ready = m.sem("var_ready")
        std_ready = m.sem("std_ready")
        shift_ready = m.sem("shift_ready")
        const_ready = m.sem("const_ready")
        A_ready = m.sem("A_ready")
        input_ready = m.sem("input_ready")
        mix_ready = m.sem("mix_ready")
        mix_taken = m.sem("mix_taken")
        S_ready = m.sem("S_ready")
        apply_ready = m.sem("apply_ready")
        xm_high = m.sem("xm_high")
        xm_split = m.sem("xm_split")
        U_ready = m.sem("U_ready")
        U_taken = m.sem("U_taken")
        GA_ready = m.sem("GA_ready")
        AGA_ready = m.sem("AGA_ready")
        square_ready = m.sem("square_ready")
        plane_ready = m.sem("plane_ready")
        plane_taken = m.sem("plane_taken")
        plane_split = m.sem("norm_plane_split")
        planes_stored = m.sem("layer_0_planes_stored")
        zeroed = m.sem("plane_zeroed")
        zeros_stored = m.sem("zeros_stored")
        centered = m.sem("centered")
        x1_ready = [m.sem(f"x1_ready{i}") for i in range(2)]
        x1_copied = m.sem("x1_copied")
        chain = m.sem("vector_chain")

        block = m.stack.enter_context(nc.Block())
        BANKS = MODES // MB

        PIECES = 4 * B

        def piece(t):
            b, q = divmod(t, 4)
            return xm[0:C, b, :, :, :].rearrange("c x r y -> c (x r y)")[:, q * 512:(q + 1) * 512]

        def pieces_of(bank):
            return range(bank * PIECES // BANKS, (bank + 1) * PIECES // BANKS)

        def plane_slots(t):
            plane, q = divmod(t, K0 // XB)
            return [plane_parts[:, plane, part, q * XB:(q + 1) * XB, :] for part in range(2)]

        @block.sync
        def _(sp):
            for b in range(B):
                sp.dma_start(xm[0:C, b, :, :, :], modes_x[b]).then_inc(modes_landed, 16)
                sp.dma_start(xm[C:, b, 0:K0, :, :], modes_x[b, :, 0:K0]).then_inc(modes_landed, 16)
            for k in range(MODES // MC):
                if k >= 2:
                    sp.wait_ge(mix_ready, (k - 1) * MC // MB)
                for r in range(2):
                    sp.dma_start(
                        weights[k % 2][r * C:(r + 1) * C, :, :],
                        w["conv"][r].rearrange("x y i o -> i (x y) o")[:, k * MC:(k + 1) * MC, :],
                    ).then_inc(weights_landed[k % 2], 16)
            sp.wait_ge(mix_ready, BANKS)
            for f in range(2):
                sp.dma_start(fw_slot(fw_first, f), fw_chunk(fw[f], 0)).then_inc(fw_landed, 16)
            for g in range(2):
                for first, row, plane in ((0, COS_0, g), (1, SIN_0, g + 1)):
                    sp.wait_ge(plane_split, 2 * (plane + 1))
                    for part in range(2):
                        sp.dma_start(planes_d[:, part, g, 0:K0, row:row + K0 - first, :].rearrange("b y k c -> b y (k c)"),
                                     plane_parts[:, plane, part, first:, :].rearrange("p k c -> p (k c)"),
                                     ).then_inc(planes_stored, 16)
            for b in range(B):
                sp.wait_ge(x1_ready[b % 2], b // 2 + 1)
                sp.dma_start(xm[C:2 * C, b, :, :, :], xm[0:C, b, :, :, :]).then_inc(x1_copied, 16)
            sp.wait_ge(x1_copied, 16 * B)
            sp.wait_ge(planes_stored, 16 * 8)
            sp.wait_ge(fw_landed, 32)

        @block.gpsimd
        def _(pool):
            nc.gpsimd.memset(zeros[:, :], 0.0).then_inc(zeroed, 1)
            pool.wait_ge(zeroed, 1)
            for d, other in ((slice(0, C), slice(C, P)), (slice(C, P), slice(0, C))):
                nc.gpsimd.memset(apply[d, :, :, other], 0.0).then_inc(zeroed, 1)
            pool.wait_ge(zeroed, 3)
            for part in range(2):
                for g in range(2):
                    pool.dma_start(planes_d[:, part, g, K0:K1, COS_0:ROWS, :].rearrange("b y k c -> b y (k c)"),
                                   zeros[:, :]).then_inc(zeros_stored, 16)
            for t in range(6):
                pool.wait_ge(plane_taken, 2 * (t + 1))
                high, low = plane_slots(t)
                nc.gpsimd.tensor_tensor(low, planes[t % 2][:, :, :], high, ALU.subtract).then_inc(plane_split, 1)
            pool.wait_ge(zeros_stored, 16 * 4)

        @block.scalar
        def _(act):
            for n in range(2):
                act.wait_ge(var_ready, n + 1)
                nc.scalar.activation(std[0:P >> n, :], var[0:P >> n, :], ACT.Sqrt).then_inc(std_ready, 1)
                if n == 1:
                    act.wait_ge(centered, 1)
                    for b in range(1, B, 2):
                        v = xm[0:C, b, :, :, :].rearrange("p x r y -> p (x r y)")
                        nc.scalar.activation(v, v, ACT.Copy, scale=rstd[0:C, b:b + 1]).then_inc(x1_ready[1], 1)
                    break
                def high(t):
                    nc.scalar.activation(xm_parts[t % 2][:, 0, :], piece(t), ACT.Copy, scale=1 / 16).then_inc(xm_high, 1)

                high(0)
                high(1)
                act.wait_ge(input_ready, 1)
                for t in range(PIECES):
                    act.wait_ge(U_ready, t + 1)
                    nc.scalar.activation(piece(t), ps_apply[t % 2][0:C, :], ACT.Copy).then_inc(U_taken, 1)
                    if t + 2 < PIECES:
                        high(t + 2)
                for t in range(6):
                    act.wait_ge(plane_ready, t + 1)
                    if t >= 2:
                        act.wait_ge(plane_split, t - 1)
                    for dst in (plane_slots(t)[0], planes[t % 2][:, :, :]):
                        nc.scalar.activation(dst, ps_plane[t % 2][0:B * K0, :, :], ACT.Copy).then_inc(plane_taken, 1)

        @block.vector
        def _(dve):
            count = [0]

            def step(ins):
                count[0] += 1
                ins.then_inc(chain, 1)
                dve.wait_ge(chain, count[0])

            def norm(n, rows):
                dve.wait_ge(means_ready, n + 1)
                step(nc.vector.tensor_copy(means[0:rows, :, :].rearrange("p s b -> p (s b)"), ps_small[0:rows, 0:2 * B]))
                step(nc.vector.tensor_tensor(var[0:rows, :], means[0:rows, 0, :], means[0:rows, 0, :], ALU.mult))
                step(nc.vector.tensor_tensor(var[0:rows, :], means[0:rows, 1, :], var[0:rows, :], ALU.subtract))
                nc.vector.tensor_scalar(var[0:rows, :], var[0:rows, :], 0.0, EPS, ALU.max, ALU.add).then_inc(var_ready, 1)
                dve.wait_ge(std_ready, n + 1)
                step(nc.vector.reciprocal(rstd[0:rows, :], std[0:rows, :]))
                step(nc.vector.tensor_tensor(std[0:rows, :], rstd[0:rows, :], rstd[0:rows, :], ALU.mult))
                step(nc.vector.tensor_tensor(std[0:rows, :], std[0:rows, :], var[0:rows, :], ALU.mult))
                step(nc.vector.tensor_scalar(std[0:rows, :], std[0:rows, :], -0.5, 1.5, ALU.mult, ALU.add))
                step(nc.vector.tensor_tensor(rstd[0:rows, :], rstd[0:rows, :], std[0:rows, :], ALU.mult))
                nc.vector.scalar_tensor_tensor(out=shift[0:rows, :], in0=means[0:rows, 0, :], scalar=-1.0,
                                               in1=rstd[0:rows, :], op0=ALU.mult, op1=ALU.mult).then_inc(shift_ready, 1)
                dve.wait_ge(shift_ready, n + 1)

            dve.wait_ge(products_ready, 1)
            step(nc.vector.tensor_copy(products[:, :, :].rearrange("p b c -> p (b c)"), ps_products[:, 0:B * C]))
            for b in range(B):
                ins = nc.vector.tensor_tensor(scratch[:, b, :], products[:, b, :], w["eye_twice"][:, :], ALU.mult)
            step(ins)
            step(nc.vector.tensor_reduce(sums[:, 1, :], scratch[:, :, :], AX.X, ALU.add))
            step(nc.vector.tensor_scalar(sums[:, 1, :], sums[:, 1, :], 1 / N / N, None, ALU.mult))
            dve.wait_ge(modes_landed, 32 * B)
            nc.vector.tensor_scalar(sums[:, 0, :], xm[:, :, 0, 0, 0], 1 / N, None, ALU.mult).then_inc(sums_ready, 1)
            norm(0, P)
            for b in range(B):
                ins = nc.vector.scalar_tensor_tensor(out=A[:, b, :], in0=w["skip"][:, :], scalar=rstd[:, b:b + 1],
                                                     in1=w["eye_twice"][:, :], op0=ALU.mult, op1=ALU.add)
            ins.then_inc(A_ready, 1)
            for b in range(B):
                for d in range(2):
                    rows = slice(d * C, (d + 1) * C)
                    for r in range(2):
                        src = xm[rows, b, 0:K0, r if d == 0 else 1 - r, 0:K0]
                        dst = mixed_in[rows, :, r, b].rearrange("p (x y) -> p x y", x=K0)
                        nc.vector.tensor_scalar(dst, src, rstd[rows, b:b + 1], -1.0 if (d, r) == (1, 0) else 1.0,
                                                ALU.mult, ALU.mult)
            dve.wait_ge(const_ready, 1)
            step(nc.vector.tensor_scalar(const[:, :], ps_small[0:C, 64:64 + B], w["skip_bias"][:, 0:1], float(N),
                                         ALU.add, ALU.mult))
            for d in range(2):
                rows = slice(d * C, (d + 1) * C)
                ins = nc.vector.scalar_tensor_tensor(out=mixed_in[rows, 0, d, :], in0=shift[rows, :], scalar=float(N),
                                                     in1=mixed_in[rows, 0, d, :], op0=ALU.mult, op1=ALU.add)
                step(ins)
            dve.sem_inc(input_ready, 1)
            halves = [slice(0, C), slice(C, P)]
            for d in halves:
                ins = nc.vector.tensor_scalar(apply[d, :, 0, d], A[d, :, :], 16.0, None, ALU.mult)
            step(ins)
            for d in halves:
                nc.vector.scalar_tensor_tensor(out=apply[d, :, 1, d], in0=A[d, :, :], scalar=16.0,
                                               in1=apply[d, :, 0, d], op0=ALU.mult,
                                               op1=ALU.subtract).then_inc(apply_ready, 1)
            dve.wait_ge(GA_ready, 1)
            nc.vector.tensor_tensor(scratch[0:C, :, :].rearrange("p b c -> p (b c)"), ps_products[0:C, 0:B * C],
                                    A[0:C, :, :].rearrange("p b c -> p (b c)"), ALU.mult).then_inc(AGA_ready, 1)
            for t in range(BANKS):
                for n in pieces_of(t):
                    dve.wait_ge(xm_high, n + 1)
                    v = xm_parts[n % 2]
                    nc.vector.scalar_tensor_tensor(out=v[:, 1, :], in0=piece(n), scalar=1 / 16, in1=v[:, 0, :],
                                                   op0=ALU.mult, op1=ALU.subtract).then_inc(xm_split, 1)
                dve.wait_ge(mix_ready, t + 1)
                v = ps_mix[t % 2][0:C, 0:MB * 2 * B].rearrange("p (k r b) -> p k r b", r=2, b=B)
                for r in range(2):
                    for x0 in range(MB // K0):
                        modes = v[:, x0 * K0:(x0 + 1) * K0, r, :].rearrange("p k b -> p b k")
                        nc.vector.tensor_copy(S[:, r, t * MB // K0 + x0, :, :], modes)
                        ins = nc.vector.tensor_scalar(S_weighted[:, r, t * MB // K0 + x0, :, :], modes, 2.0, None, ALU.mult)
                ins.then_inc(mix_taken, 1)
            dve.wait_ge(mix_taken, BANKS)
            step(nc.vector.tensor_tensor(S[:, 0, 0, :, 0], S[:, 0, 0, :, 0], const[:, :], ALU.add))
            dve.sem_inc(S_ready, 1)

            def flat(t):
                return t[:, :, :, :, :].rearrange("p r x b y -> p (r x b y)")
            step(nc.vector.tensor_copy(S_weighted[:, :, :, :, 0], S[:, :, :, :, 0]))
            step(nc.vector.tensor_scalar(flat(S_real), flat(S_weighted), 0.5, None, ALU.mult))
            nc.vector.tensor_copy(S_real[:, 0, 0, :, 0], S[:, 0, 0, :, 0])
            step(nc.vector.memset(S_real[:, 1, 0, :, 0], 0.0))
            dve.wait_ge(U_taken, 4 * B)
            for b in range(B):
                for r in range(2):
                    ins = nc.vector.tensor_tensor(xm[0:C, b, 0:K0, r, 0:K0], xm[0:C, b, 0:K0, r, 0:K0],
                                                  S_real[:, r, :, b, :], ALU.add)
            step(ins)
            for b in range(B):
                for r in range(2):
                    ins = nc.vector.scalar_tensor_tensor(out=S_real[:, r, :, b, :], in0=xm[0:C, b, 0:K0, r, 0:K0],
                                                         scalar=2.0, in1=S_real[:, r, :, b, :], op0=ALU.mult,
                                                         op1=ALU.subtract)
            step(ins)
            step(nc.vector.tensor_tensor(flat(S_real), flat(S_real), flat(S_weighted), ALU.mult))
            step(nc.vector.tensor_reduce(cross_sum[:, :], S_real[:, :, :, :, :].rearrange("p r x b y -> p b (r x) y"),
                                         AX.XY, ALU.add))
            dve.wait_ge(square_ready, 1)
            step(nc.vector.tensor_tensor(cross_sum[:, :], cross_sum[:, :], ps_small[0:C, 128:128 + B], ALU.add))
            nc.vector.tensor_scalar(sums[0:C, 0, :], xm[0:C, :, 0, 0, 0], 1 / N, None, ALU.mult).then_inc(sums_ready, 1)
            nc.vector.tensor_scalar(sums[0:C, 1, :], cross_sum[:, :], 1 / N / N, None, ALU.mult).then_inc(sums_ready, 1)
            norm(1, C)
            nc.vector.scalar_tensor_tensor(out=xm[0:C, :, 0, 0, 0], in0=means[0:C, 0, :], scalar=float(-N),
                                           in1=xm[0:C, :, 0, 0, 0], op0=ALU.mult, op1=ALU.add).then_inc(centered, 1)
            dve.wait_ge(centered, 1)
            for b in range(0, B, 2):
                v = xm[0:C, b, :, :, :].rearrange("p x r y -> p (x r y)")
                nc.vector.tensor_scalar(v, v, rstd[0:C, b:b + 1], None, ALU.mult).then_inc(x1_ready[0], 1)

        @block.tensor
        def _(pe):
            nc.tensor.matmul(ps_products[:, 0:B * C], w["sum_parts"][:, :],
                             gram[:, :, :].rearrange("p b c -> p (b c)"), start=True, stop=True).then_inc(products_ready, 1)
            pe.wait_ge(sums_ready, 1)
            nc.tensor.matmul(ps_small[:, 0:2 * B], w["pair_mean"][:, :], sums[:, :, :].rearrange("p s b -> p (s b)"),
                             start=True, stop=True).then_inc(means_ready, 1)
            pe.wait_ge(shift_ready, 1)
            nc.tensor.matmul(ps_small[0:C, 64:64 + B], w["skip"][0:C, :], shift[0:C, :],
                             start=True, stop=True).then_inc(const_ready, 1)
            pe.wait_ge(A_ready, 1)
            for b in range(B):
                last = nc.tensor.matmul(ps_products[0:C, b * C:(b + 1) * C], products[0:C, b, :], A[0:C, b, :],
                                        start=True, stop=True)
            last.then_inc(GA_ready, 1)
            def apply_to_modes(t):
                b = t // 4
                if t == 0:
                    pe.wait_ge(apply_ready, 2)
                if t >= 2:
                    pe.wait_ge(U_taken, t - 1)
                pe.wait_ge(xm_split, t + 1)
                for n, (p, q) in enumerate(((0, 0), (0, 1), (1, 0))):
                    last = nc.tensor.matmul(ps_apply[t % 2][0:C, :], apply[0:C, b, q, 0:C], xm_parts[t % 2][:, p, :],
                                            start=(n == 0), stop=(n == 2))
                last.then_inc(U_ready, 1)

            pe.wait_ge(input_ready, 1)
            for t in range(BANKS):
                k = t * MB // MC
                if t * MB % MC == 0:
                    pe.wait_ge(weights_landed[k % 2], 32 * (k // 2 + 1))
                if t >= 2:
                    pe.wait_ge(mix_taken, t - 1)
                for j in range(MB):
                    mode = t * MB + j
                    last = nc.tensor.matmul(ps_mix[t % 2][0:C, j * 2 * B:(j + 1) * 2 * B],
                                            weights[k % 2][:, mode % MC, :],
                                            mixed_in[:, mode, :, :].rearrange("p r b -> p (r b)"),
                                            start=True, stop=True)
                    if j == MB - 1:
                        last.then_inc(mix_ready, 1)
                    pieces = pieces_of(t)
                    for n in pieces:
                        if j == (n - pieces[0] + 1) * MB // len(pieces) - 1:
                            apply_to_modes(n)
            pe.wait_ge(AGA_ready, 1)
            for b in range(B):
                last = nc.tensor.matmul(ps_small[0:C, 128 + b:129 + b], scratch[0:C, b, :], w["ones"][0:C, 0:1],
                                        start=True, stop=True)
            last.then_inc(square_ready, 1)
            pe.wait_ge(S_ready, 1)
            for t in range(6):
                plane, q = divmod(t, K0 // XB)
                if t >= 2:
                    pe.wait_ge(plane_taken, 2 * (t - 1))
                r, eye = ((0, "eye"), (1, "eye"), (0, "minus_eye"))[plane]
                for x in range(XB):
                    last = nc.tensor.matmul(ps_plane[t % 2][0:B * K0, x, :],
                                            S[:, r, q * XB + x, :, :].rearrange("c b y -> c (b y)"), w[eye][0:C, 0:C],
                                            start=True, stop=True)
                last.then_inc(plane_ready, 1)
            pe.wait_ge(sums_ready, 3)
            nc.tensor.matmul(ps_small[0:C, 0:2 * B], w["pair_mean"][0:C, 0:C], sums[0:C, :, :].rearrange("p s b -> p (s b)"),
                             start=True, stop=True).then_inc(means_ready, 1)


def mixing_1(nc, B, x1_modes, fw, fw_first, mixed):
    SL = 2
    MG = K1 // 4
    R = 2 * 2 * B
    with Memory(nc) as m:
        weights = [fw_first] + [m.sb(f"fw{i}", [P, C, KC, 2 * K1]) for i in range(1, SL)]
        blocks = [m.sb(f"blocks{i}", [P, 2, B, 2, K1]) for i in range(2)]
        out = [m.sb(f"mix_out{i}", [P, MG, 2 * C]) for i in range(2)]
        zeros = m.sb("mix_zeros", [2 * B, K1 * 2 * C])
        ps = [[m.ps(f"mix_ps{i}{h}", [P, MG // 2, 2 * C]) for h in range(2)] for i in range(2)]

        landed = [m.sem(f"fw_landed{i}") for i in range(SL)]
        zeroed = m.sem("zeroed")
        zeros_stored = m.sem("mix_zeros_stored")
        placed = m.sem("placed")
        ready = m.sem("mix1_ready")
        taken_low = m.sem("mix1_taken_low")
        taken_high = m.sem("mix1_taken_high")
        stored = [m.sem(f"mix1_stored{i}") for i in range(2)]
        block = m.stack.enter_context(nc.Block())
        TURN = 8
        AHEAD = SL * KC
        assert TURN // KC % SL == 0

        @block.sync
        def _(sp):
            def load(t, i):
                at = sp.snap((t * (TURN // KC) + i) * (KC * 2 * K1))
                sp.wait_ge(ready, t * TURN + (i + 1) * KC)
                for f in range(2):
                    sp.dma_start(fw_slot(weights[i % SL], f), fw_chunk(fw[f], at)).then_inc(landed[i % SL], 16)

            sp.sem_inc(landed[0], 32)
            with sp.Fori(0, K1 // TURN - 1) as t:
                for i in range(TURN // KC):
                    load(t, i + 1)
            for i in range(TURN // KC - 1):
                at = (K1 - TURN + (i + 1) * KC) * 2 * K1
                sp.wait_ge(ready, K1 - TURN + (i + 2) * KC)
                for f in range(2):
                    slot = (i + 1) % SL
                    sp.dma_start(fw_slot(weights[slot], f), fw_chunk(fw[f], at)).then_inc(landed[slot], 16)

        @block.gpsimd
        def _(pool):
            for i in range(2):
                nc.gpsimd.memset(blocks[i][:, :, :, :, :], 0.0).then_inc(zeroed, 1)
            nc.gpsimd.memset(zeros[:, :], 0.0).then_inc(zeroed, 1)
            pool.wait_ge(zeroed, 3)
            for f, x in ((0, K1 // TURN), (1, 0)):
                pool.dma_start(mixed[f, :, :, x, :, 0, :].rearrange("b r y w -> (b r) y w"),
                               zeros[:, :].rearrange("p (y w) -> p y w", w=2 * C)).then_inc(zeros_stored, 16)
            with pool.Fori(0, K1 // TURN) as t:
                for i in range(TURN):
                    pool.wait_ge(ready, t * TURN + i + 1 + AHEAD - 2)
                    for f in range(2):
                        rows = slice(f * C, (f + 1) * C)
                        nc.gpsimd.tensor_copy(blocks[i % 2][rows, f, :, :, :].rearrange("p b r y -> p b (r y)"),
                                              x1_modes[rows, :, bass.ds(t * TURN + i, 1), :, :]
                                              .rearrange("p b o r y -> p b (o r y)")).then_inc(placed, 1)
            pool.wait_ge(zeros_stored, 32)

        @block.tensor
        def _(pe):
            pe.sem_inc(ready, AHEAD)
            with pe.Fori(0, K1 // TURN) as t:
                for i in range(TURN):
                    if i % KC == 0:
                        chunk = i // KC
                        pe.wait_ge(landed[chunk % SL], 32 * (t * (TURN // AHEAD) + chunk // SL + 1))
                    pe.wait_ge(placed, 2 * (t * TURN + i + 1))
                    pe.wait_ge(taken_low, t * TURN + i + 1)
                    pe.wait_ge(taken_high, t * TURN + i + 1)
                    for h in range(2):
                        for g in range(h * MG // 2, (h + 1) * MG // 2):
                            for j in range(4):
                                y = MG * j + g
                                last = nc.tensor.matmul(
                                    ps[i % 2][h][32 * j:32 * j + R, g % (MG // 2), :],
                                    blocks[i % 2][:, :, :, :, y].rearrange("p f b r -> p (f b r)"),
                                    weights[i // KC % SL][:, :, i % KC, 2 * y:2 * y + 2],
                                    start=True, stop=True, tile_position=(0, 32 * j))
                    last.then_inc(ready, 1)

        def quadrants():
            return [slice(32 * j, 32 * j + R) for j in range(4)] if R < 32 else [slice(0, P)]

        @block.scalar
        def _(act):
            act.sem_inc(taken_low, 2)
            for i in range(2):
                act.sem_inc(stored[i], 1)
            with act.Fori(0, K1 // TURN) as t:
                for i in range(TURN):
                    x = t * TURN + i
                    act.wait_ge(ready, x + 1 + AHEAD)
                    act.wait_ge(stored[i % 2], t * (128 * TURN // 2) + 128 * (i // 2) + 1)
                    for rows in quadrants():
                        last = nc.scalar.activation(out[i % 2][rows, 0:MG // 2, :], ps[i % 2][0][rows, :, :], ACT.Copy)
                    last.then_inc(taken_low, 1)
                    act.wait_ge(taken_low, x + 3)
                    act.wait_ge(taken_high, x + 3)
                    for f in range(2):
                        k, q = (t, i) if f == 0 else (K1 // TURN - (i > 0) - t, -i % TURN)
                        for j in range(4):
                            act.dma_start(
                                mixed[f].rearrange("b r x y q w -> (b r) x y q w")
                                [:, bass.ds(k, 1), j * MG:(j + 1) * MG, q, :].rearrange("p o y w -> p (o y) w"),
                                out[i % 2][32 * j + f * R // 2:32 * j + (f + 1) * R // 2, :, :],
                                ).then_inc(stored[i % 2], 16)
            for i in range(2):
                act.wait_ge(stored[i], 128 * (K1 // 2) + 1)

        @block.vector
        def _(dve):
            dve.sem_inc(taken_high, 2)
            with dve.Fori(0, K1 // TURN) as t:
                for i in range(TURN):
                    x = t * TURN + i
                    dve.wait_ge(ready, x + 1 + AHEAD)
                    dve.wait_ge(stored[i % 2], t * (128 * TURN // 2) + 128 * (i // 2) + 1)
                    for rows in quadrants():
                        last = nc.vector.tensor_copy(out[i % 2][rows, MG // 2:, :], ps[i % 2][1][rows, :, :])
                    last.then_inc(taken_high, 1)


PROJECT_SCALE = 1.0 / (N * float(np.sqrt(np.float32(N * (N // 2 + 1)))))


def project_1(nc, B, mixed, planes_d, w):
    Q = K1 // 4 + 1
    STEP = 3
    STEPS = 2 * Q // STEP
    LOADS = 4
    STORES = 11
    with Memory(nc) as m:
        raw = [m.sb(f"raw{i}", [P, 2, 2, Q, C, 2]) for i in range(2)]
        T = [m.sb(f"T{f}", [P, Q, 2, C]) for f in range(2)]
        GH = [m.sb(f"GH{i}", [P, Q, 2, 2, C]) for i in range(2)]
        turned = [m.sb(f"turned{i}", [P, STEP, P]) for i in range(2)]
        out = [m.sb(f"project_out{i}", [P, 2, 2, 2, Q, C], F16) for i in range(2)]
        ps_turn = [m.ps(f"ps_turn{i}", [P, STEP, P]) for i in range(2)]
        ps_out = [m.ps(f"ps_out{i}", [P, STEP, 2, C]) for i in range(4)]

        cleared = m.sem("raw_cleared")
        landed = [m.sem(f"raw_landed{i}") for i in range(2)]
        combined = m.sem("combined")
        summed = m.sem("summed")
        turn_ready = m.sem("turn_ready")
        turn_taken = m.sem("turn_taken")
        out_ready = m.sem("out_ready")
        out_high = m.sem("out_high")
        out_taken = m.sem("out_taken")
        stored = [m.sem(f"planes_stored{i}") for i in range(2)]
        block = m.stack.enter_context(nc.Block())

        def out_slots(b, s):
            h, q = divmod(s * STEP, Q)
            return [out[b % 2][:, h, part, :, q:q + STEP, :] for part in range(2)]

        @block.sync
        def _(sp):
            def load(b):
                v = raw[b % 2]
                for f in range(2):
                    src = mixed[f, b].rearrange("r x y q w -> (x y) r (q w)")
                    sp.dma_start(v[:, f, :, 0:Q - 1, :, :].rearrange("p r k o w -> p r (k o w)"),
                                 src[0:P]).then_inc(landed[b % 2], 16)
                    sp.dma_start(v[0:K1, f, :, Q - 1, :, :].rearrange("p r o w -> p r (o w)"),
                                 src[P:, :, 0:2 * C]).then_inc(landed[b % 2], 16)

            for b in range(min(B, 2)):
                sp.wait_ge(cleared, b + 1)
                load(b)
            for b in range(B):
                if b + 2 < B:
                    sp.wait_ge(combined, 4 * (b + 1))
                    load(b + 2)
                sp.wait_ge(out_taken, (b + 1) * STEPS)
                v = out[b % 2]
                dst = planes_d[b].rearrange("q g y k c -> y (q g) (k c)")
                PX = (Q - 1) * C
                G, H = (v[:, h, :, :, :, :].rearrange("p q g k c -> p (q g) (k c)") for h in range(2))
                stores = [
                    (dst[:, :, K1 * C:SIN_1 * C], G[0:K1, :, PX:]),
                    (dst[:, :, SIN_1 * C:SIN_1 * C + PX - C], H[0:K1, :, C:PX]),
                    (dst[:, :, (ROWS_1 - 1) * C:ROWS_1 * C], H[0:K1, :, PX:])]
                for g in range(4):
                    stores.append((dst[:, g, 0:4 * PX].rearrange("y (x k) -> x y k", x=4), G[:, g, 0:PX]))
                    stores.append((dst[:, g, SIN_1 * C + PX - C:SIN_1 * C + 4 * PX - C]
                                   .rearrange("y (x k) -> x y k", x=3), H[K1:, g, 0:PX]))
                for rows, src in stores:
                    sp.dma_start(rows, src).then_inc(stored[b % 2], 16)
            for i in range(min(B, 2)):
                sp.wait_ge(stored[i], 16 * STORES * ((B - i + 1) // 2))

        @block.vector
        def _(dve):
            def combine(b):
                dve.wait_ge(landed[b % 2], 16 * LOADS * (b // 2 + 1))
                v = raw[b % 2]
                if b >= 1:
                    dve.wait_ge(summed, 2 * b)
                for f in range(2):
                    nc.vector.tensor_tensor(T[f][:, :, 0, :], v[:, f, 0, :, :, 0], v[:, f, 1, :, :, 1],
                                            ALU.subtract).then_inc(combined, 1)
                    nc.vector.tensor_tensor(T[f][:, :, 1, :], v[:, f, 0, :, :, 1], v[:, f, 1, :, :, 0],
                                            ALU.add).then_inc(combined, 1)

            def add_up(b):
                dve.wait_ge(combined, 4 * (b + 1))
                if b >= 2:
                    dve.wait_ge(turn_ready, (b - 1) * STEPS)
                for h, op in enumerate((ALU.add, ALU.subtract)):
                    nc.vector.tensor_tensor(GH[b % 2][:, :, h, :, :].rearrange("p q r c -> p q (r c)"),
                                            T[0][:, :, :, :].rearrange("p q r c -> p q (r c)"),
                                            T[1][:, :, :, :].rearrange("p q r c -> p q (r c)"), op).then_inc(summed, 1)

            for i in range(2):
                nc.vector.memset(raw[i][:, :, :, Q - 1, :, :].rearrange("p f r o w -> p (f r) (o w)"),
                                 0.0).then_inc(cleared, 1)
            dve.wait_ge(cleared, 2)
            combine(0)
            add_up(0)
            for b in range(B):
                for s in range(STEPS):
                    n = b * STEPS + s
                    dve.wait_ge(out_high, n + 1)
                    high, low = out_slots(b, s)
                    for g in range(2):
                        last = nc.vector.scalar_tensor_tensor(out=low[:, g], in0=ps_out[n % 4][:, :, g, :],
                                                              scalar=PROJECT_SCALE, in1=high[:, g], op0=ALU.mult,
                                                              op1=ALU.subtract)
                    last.then_inc(out_taken, 1)
                    if s == 0 and b + 1 < B:
                        combine(b + 1)
                    if s == 1 and b + 1 < B:
                        add_up(b + 1)

        @block.tensor
        def _(pe):
            def turn(n):
                b, s = divmod(n, STEPS)
                if s == 0:
                    pe.wait_ge(summed, 2 * (b + 1))
                if n >= 2:
                    pe.wait_ge(turn_taken, n - 1)
                for j in range(STEP):
                    h, q = divmod(s * STEP + j, Q)
                    last = nc.tensor.transpose(ps_turn[n % 2][:, j, :],
                                               GH[b % 2][:, q, h, :, :].rearrange("p r c -> p (r c)"), w["eye"][:, :])
                last.then_inc(turn_ready, 1)

            turn(0)
            for n in range(B * STEPS):
                if n + 1 < B * STEPS:
                    turn(n + 1)
                pe.wait_ge(turn_taken, n + 1)
                if n >= 4:
                    pe.wait_ge(out_taken, n - 3)
                for j in range(STEP):
                    h = (n % STEPS * STEP + j) // Q
                    first = n % STEPS == 0 and j == 0
                    last = nc.tensor.matmul(ps_out[n % 4][:, j, :, :].rearrange("p a c -> p (a c)"),
                                            turned[n % 2][:, j, :], w["project"][:, h, :], start=True, stop=not first)
                    if first:
                        nc.tensor.matmul(ps_out[n % 4][:, 0, 0, :], w["eye"][0:1, :], w["bias_n"][0:1, :],
                                         start=False, stop=True)
                last.then_inc(out_ready, 1)

        @block.scalar
        def _(act):
            def take_turn(n):
                act.wait_ge(turn_ready, n + 1)
                if n >= 2:
                    act.wait_ge(out_ready, n - 1)
                nc.scalar.activation(turned[n % 2][:, :, :], ps_turn[n % 2][:, :, :], ACT.Copy).then_inc(turn_taken, 1)

            take_turn(0)
            for n in range(B * STEPS):
                b, s = divmod(n, STEPS)
                if n + 1 < B * STEPS:
                    take_turn(n + 1)
                if b >= 2 and s == 0:
                    act.wait_ge(stored[b % 2], 16 * STORES * (b // 2))
                act.wait_ge(out_ready, n + 1)
                nc.scalar.activation(out_slots(b, s)[0], ps_out[n % 4][:, :, :, :].rearrange("p j g c -> p g j c"),
                                     ACT.Copy, scale=PROJECT_SCALE).then_inc(out_high, 1)


COS_1, SIN_1 = 0, K1 + 1
ROWS_1 = 2 * K1 + 1
COS_0, SIN_0 = ROWS_1, ROWS_1 + K0
ROWS = ROWS_1 + 2 * K0 - 1
AGAIN = ROWS
R0 = ROWS - ROWS_1
TILE_0 = 3 * R0 - 1
WB = 128
BLOCKS = N // WB
COPIES = 4
W2 = 32
UW = 8
UNITS = W2 // UW
CHUNKS = HALVES * N // W2
U = CHUNKS * UNITS
UB = U // BLOCKS
X_SLOTS = 4
Y_SLOTS = 4
GC = 4
GROUPS_2 = C // GC


def pass_2(nc, B, x, y, apply, planes, w):
    with Memory(nc) as m:
        D = m.sb("planes_in", [P, P, C], F16)
        high_tile = [m.sb(f"high_tile{t}", [P, WB, C], F16) for t in range(BLOCKS)]
        low_tile = [m.sb(f"low_tile{t}", [P, WB, C], F16) for t in range(BLOCKS)]
        tile_0 = [m.sb(f"tile_0{t}", [TILE_0, WB, C], F16) for t in range(BLOCKS)]
        x_in = [m.sb(f"x_in{i}", [P, W2, C]) for i in range(X_SLOTS)]
        turned = [m.sb(f"x_turned{i}", [P, 2, UW // 2, P], F16) for i in range(2)]
        relu = [m.sb(f"relu{i}", [P, UW, C]) for i in range(2)]
        y_out = [m.sb(f"y_out{i}", [P, W2, C]) for i in range(Y_SLOTS)]
        ps_col = [m.ps(f"ps_col{i}", [P, GC, WB]) for i in range(2)]
        ps_turn = [m.ps(f"ps_xt{i}", [P, UW // 2, P]) for i in range(2)]
        ps_y = [m.ps(f"ps_y{i}", [P, UW, C]) for i in range(2)]
        ps_wave = [m.ps(f"ps_wave{i}", [P, UW, C]) for i in range(2)]

        planes_landed = m.sem("planes_landed")
        col_ready = m.sem("col_ready")
        col_high = m.sem("col_high")
        col_taken = m.sem("col_taken")
        tiles_filled = m.sem("tiles_filled")
        x_landed = [m.sem(f"x_landed{i}") for i in range(X_SLOTS)]
        turn_ready = m.sem("x_turn_ready")
        turn_high = m.sem("x_turn_high")
        turn_split = m.sem("x_turn_split")
        wave_ready = m.sem("wave_ready")
        relu_ready = m.sem("relu_ready")
        y_ready = m.sem("y_ready")
        y_done = m.sem("y_done")
        y_stored = [m.sem(f"y_stored{i}") for i in range(Y_SLOTS)]
        block = m.stack.enter_context(nc.Block())

        def chunk_at(ch):
            return ch // HALVES, ch % HALVES

        def group_of(u):
            t, g = divmod(u, UB)
            return (t == 1, 1 - t, g) if g < GROUPS_2 else None

        def group_number(b, t, g):
            return (b * BLOCKS + t) * GROUPS_2 + g

        @block.sync
        def _(sp):
            def load(b, ch):
                wq, hh = chunk_at(ch)
                sp.wait_ge(turn_ready, (b * CHUNKS + ch + 1) * UNITS)
                sp.dma_start(x_in[ch % X_SLOTS][:, :, :],
                             x[bass.ds(b, 1), hh * P:(hh + 1) * P, wq * W2:(wq + 1) * W2, :]
                             .rearrange("o h w c -> h (o w) c")).then_inc(x_landed[ch % X_SLOTS], 16)

            def load_planes(b):
                v = planes[bass.ds(b, 1)].rearrange("o q g y k c -> (o q g y) k c")
                sp.dma_start(D[:, 0:ROWS, :], v).then_inc(planes_landed, 16)
                sp.dma_start(D[:, AGAIN:, :], v[:, COS_1 + 1:SIN_1, :]).then_inc(planes_landed, 16)

            def fill_tiles(b, t):
                sp.wait_ge(col_taken, group_number(b, t, GROUPS_2 - 1) + 3)
                high, low, zero = high_tile[t], low_tile[t], tile_0[t]
                for dst, src in ((low[AGAIN:], high[SIN_1:ROWS_1]), (zero[0:R0], high[COS_0:ROWS]),
                                 (zero[R0:2 * R0], low[COS_0:ROWS]), (zero[2 * R0:], high[COS_0 + 1:ROWS])):
                    sp.dma_start(dst, src).then_inc(tiles_filled, 16)

            def image(b, last):
                for ch in range(CHUNKS):
                    wq, hh = chunk_at(ch)
                    sp.wait_ge(y_done, b * U + (ch + 1) * UNITS + 2)
                    sp.dma_start(y[bass.ds(b, 1), hh * P:(hh + 1) * P, wq * W2:(wq + 1) * W2, :]
                                 .rearrange("o h w c -> h (o w) c"),
                                 y_out[ch % Y_SLOTS][:, :, :]).then_inc(y_stored[ch % Y_SLOTS], 16)
                    if ch + X_SLOTS < CHUNKS:
                        load(b, ch + X_SLOTS)
                    elif not last:
                        load(b + 1, ch + X_SLOTS - CHUNKS)
                    if (ch + 1) * UNITS == GROUPS_2:
                        fill_tiles(b, 1)
                        if not last:
                            load_planes(b + 1)
                    if (ch + 1) * UNITS == UB + GROUPS_2 and not last:
                        fill_tiles(b + 1, 0)
            for i in range(Y_SLOTS):
                sp.sem_inc(y_stored[i], 1)
            load_planes(0)
            for n in range(X_SLOTS):
                load(0, n)
            fill_tiles(0, 0)
            with sp.Fori(0, B - 1) as b:
                image(b, False)
            image(B - 1, True)
            for i in range(Y_SLOTS):
                sp.wait_ge(y_stored[i], 16 * B * CHUNKS // Y_SLOTS + 1)

        def columns_of(v, g):
            return v[:, :, g * GC:(g + 1) * GC].rearrange("p w c -> p c w")

        @block.scalar
        def _(act):
            def columns(b, t, g):
                act.wait_ge(col_ready, group_number(b, t, g) + 1)
                nc.scalar.activation(columns_of(high_tile[t], g), ps_col[g % 2][:, :, :], ACT.Copy,
                                     scale=1 / 16).then_inc(col_high, 1)

            def split(b, u):
                act.wait_ge(turn_ready, b * U + u + 1 + X_SLOTS * UNITS)
                act.wait_ge(y_ready, b * U + u + 1)
                nc.scalar.activation(turned[u % 2][:, 0, :, :], ps_turn[u % 2][:, :, :], ACT.Copy).then_inc(turn_high, 1)

            def image(b, last):
                for u in range(U):
                    if u + 1 < U:
                        split(b, u + 1)
                    elif not last:
                        split(b + 1, 0)
                    act.wait_ge(wave_ready, b * U + u + 1)
                    act.wait_ge(y_done, b * U + u + 1)
                    nc.scalar.activation(relu[u % 2][:, :, :], ps_wave[u % 2][:, :, :], ACT.Relu,
                                         scale=1 / 16).then_inc(relu_ready, 1)
                    if group_of(u):
                        ahead, t, g = group_of(u)
                        if not ahead:
                            columns(b, t, g)
                        elif not last:
                            columns(b + 1, t, g)

            act.sem_inc(relu_ready, 2)
            for g in range(GROUPS_2):
                columns(0, 0, g)
            split(0, 0)
            with act.Fori(0, B - 1) as b:
                image(b, False)
            image(B - 1, True)

        @block.vector
        def _(dve):
            dve.sem_inc(col_taken, 2)
            dve.sem_inc(turn_split, 2)
            dve.sem_inc(y_done, 2)

            def columns(b, t, g):
                dve.wait_ge(col_high, group_number(b, t, g) + 1)
                nc.vector.scalar_tensor_tensor(out=columns_of(low_tile[t], g)[0:ROWS], in0=ps_col[g % 2][0:ROWS, :, :],
                                               scalar=1 / 16, in1=columns_of(high_tile[t], g)[0:ROWS],
                                               op0=ALU.mult, op1=ALU.subtract).then_inc(col_taken, 1)

            def split(b, u):
                dve.wait_ge(turn_high, b * U + u + 1)
                v = turned[u % 2]
                nc.vector.tensor_tensor(v[:, 1, :, :], ps_turn[u % 2][:, :, :], v[:, 0, :, :],
                                        ALU.subtract).then_inc(turn_split, 1)

            def image(b, last):
                for u in range(U):
                    if u + 1 < U:
                        split(b, u + 1)
                    elif not last:
                        split(b + 1, 0)
                    ch, j = divmod(u, UNITS)
                    if group_of(u):
                        ahead, t, g = group_of(u)
                        if not ahead:
                            columns(b, t, g)
                        elif not last:
                            columns(b + 1, t, g)
                    if j == 0:
                        dve.wait_ge(y_stored[ch % Y_SLOTS], b * (16 * CHUNKS // Y_SLOTS) + 16 * (ch // Y_SLOTS) + 1)
                    dve.wait_ge(relu_ready, b * U + u + 3)
                    dve.wait_ge(y_ready, b * U + u + 3)
                    nc.vector.scalar_tensor_tensor(out=y_out[ch % Y_SLOTS][:, j * UW:(j + 1) * UW, :]
                                                   .rearrange("p w c -> p (w c)"),
                                                   in0=ps_y[u % 2][:, :, :].rearrange("p w c -> p (w c)"), scalar=1 / 16,
                                                   in1=relu[u % 2][:, :, :].rearrange("p w c -> p (w c)"),
                                                   op0=ALU.mult, op1=ALU.add).then_inc(y_done, 1)

            for g in range(GROUPS_2):
                columns(0, 0, g)
            split(0, 0)
            with dve.Fori(0, B - 1) as b:
                image(b, False)
            image(B - 1, True)

        @block.tensor
        def _(pe):
            pe.sem_inc(turn_ready, X_SLOTS * UNITS)
            pe.sem_inc(y_ready, 2)

            def turn(b, u):
                ch, j = divmod(u, UNITS)
                if j == 0:
                    pe.wait_ge(x_landed[ch % X_SLOTS], 16 * (b * (CHUNKS // X_SLOTS) + ch // X_SLOTS + 1))
                pe.wait_ge(turn_split, b * U + u + 1)
                for k in range(UW // 2):
                    at = j * UW + 2 * k
                    last = nc.tensor.transpose(ps_turn[u % 2][:, k, :], x_in[ch % X_SLOTS][:, at:at + 2, :]
                                               .rearrange("p w c -> p (w c)"), w["eye"][:, :])
                last.then_inc(turn_ready, 1)

            def columns(b, t, g):
                pe.wait_ge(col_taken, group_number(b, t, g) + 1)
                if (t, g) == (0, 0):
                    pe.wait_ge(planes_landed, 32 * (b + 1))
                for c in range(GC):
                    for q in range(2):
                        last = nc.tensor.matmul(ps_col[g % 2][:, c, :], D[:, :, g * GC + c],
                                                w["waves_w"][:, q, t * WB:(t + 1) * WB], start=(q == 0), stop=(q == 1))
                last.then_inc(col_ready, 1)

            def image(b, last):
                for u in range(U):
                    ch, j = divmod(u, UNITS)
                    wq, hh = chunk_at(ch)
                    t = u // UB
                    w0 = wq * W2 + j * UW - t * WB
                    high, low, zero = (v[t][:, w0:w0 + UW, :] for v in (high_tile, low_tile, tile_0))
                    if u + 1 < U:
                        turn(b, u + 1)
                    elif not last:
                        turn(b + 1, 0)
                    if u % UB == 0:
                        pe.wait_ge(tiles_filled, 16 * COPIES * (b * BLOCKS + t + 1))
                    pe.wait_ge(relu_ready, b * U + u + 1)
                    for q, v in enumerate((high, low)):
                        mm = nc.tensor.matmul(ps_wave[u % 2][:, :, :], w["waves_h1"][:, hh, q, :], v,
                                              start=(q == 0), stop=(q == 1))
                    mm.then_inc(wave_ready, 1)
                    pe.wait_ge(y_done, b * U + u + 1)
                    nc.tensor.matmul(ps_y[u % 2][:, :, :], w["waves_h0"][:, hh, :], zero, start=True, stop=False)
                    if group_of(u):
                        ahead, tt, g = group_of(u)
                        if not ahead:
                            columns(b, tt, g)
                        elif not last:
                            columns(b + 1, tt, g)
                    pe.wait_ge(turn_split, b * U + u + 3)
                    for k in range(UW // 2):
                        for n, (p, q) in enumerate(((0, 0), (0, 1), (1, 0))):
                            mm = nc.tensor.matmul(
                                ps_y[u % 2][:, 2 * k:2 * k + 2, :].rearrange("p w c -> p (w c)"), turned[u % 2][:, p, k, :],
                                apply[:, bass.ds(b, 1), q, :].rearrange("p o c -> p (o c)"),
                                start=False, stop=(n == 2 and k == UW // 2 - 1))
                    mm.then_inc(y_ready, 1)

            for g in range(GROUPS_2):
                columns(0, 0, g)
            turn(0, 0)
            with pe.Fori(0, B - 1) as b:
                image(b, False)
            image(B - 1, True)


def dft_constants():
    def parts(a):
        hi = a.astype(np.float16)
        return np.stack([hi, (a - hi).astype(np.float16)], -2)

    def angle(n, k):
        return 2 * np.pi * ((n[:, None] * k[None, :]) % N) / N

    t = {}
    n = np.arange(N)
    a = angle(n, np.arange(K1))
    cos, sin = np.cos(a), np.sin(a)
    e = np.concatenate([cos, -sin], 1)
    t["rows_dft"] = parts(e.reshape(HALVES, P, 2 * K1).transpose(1, 0, 2))
    e = np.stack([np.concatenate([cos, -sin], 1), np.concatenate([sin, cos], 1)], 1)
    e = e.reshape(HALVES, P, 2, 2 * K1).transpose(1, 0, 2, 3)
    hi = e.astype(np.float16)
    t["cols_dft"] = np.stack([hi, (e - hi).astype(np.float16)], 2)

    a = angle(np.arange(K1), n)
    weight = np.where(np.arange(K1) > 0, 2.0, 1.0)[:, None]
    e = np.concatenate([weight * np.cos(a), -weight * np.sin(a)], 0)
    t["waves_w"] = parts(np.concatenate([e, e], 0))
    k = np.arange(K1 + 1)
    a = angle(k, n).reshape(K1 + 1, HALVES, P)
    rows = parts(np.concatenate([np.cos(a), -np.sin(a[1:])], 0))
    high, low = rows[:, :, 0], rows[:, :, 1]
    e = np.zeros((P, HALVES, 2, P), np.float16)
    e[COS_1:ROWS_1] = high[:, :, None]
    e[AGAIN:, :, 0], e[AGAIN:, :, 1] = low[COS_1 + 1:SIN_1], low[SIN_1:]
    t["waves_h1"] = e
    high, low = (np.concatenate([v[:K0], v[SIN_1:SIN_1 + K0 - 1]], 0) for v in (high, low))
    t["waves_h0"] = np.concatenate([high, high, low[1:]], 0)
    eye = np.eye(P, dtype=np.float32)
    t["eye"] = eye
    t["minus_eye"] = -eye[:C, :C]
    t["eye_twice"] = np.concatenate([eye[:C, :C]] * 2, 0)
    t["ones"] = np.ones((P, 1), np.float32)
    c = np.arange(P)
    t["sum_parts"] = ((c[:, None] % C == c[None, :] % C) * np.where(c < C, 1, 2)[:, None]).astype(np.float32)
    t["pair_mean"] = (((c[:, None] // 2) == (c[None, :] % C) // 2) * 0.5).astype(np.float32)
    return t


def prepare(nc, w):
    with Memory(nc) as m:
        done = m.sem("prepared")
        block = m.stack.enter_context(nc.Block())

        @block.vector
        def _(dve):
            project, re, im = w["project"], slice(0, C), slice(C, 2 * C)
            nc.vector.memset(project[:, :, :], 0.0).then_inc(done, 1)
            nc.vector.tensor_scalar(w["bias_n"][:, :], w["bias"][:, :], N / PROJECT_SCALE, None, ALU.mult).then_inc(done, 1)
            dve.wait_ge(done, 2)
            for h, rows, cols in ((0, re, re), (0, im, im), (1, im, re)):
                nc.vector.tensor_tensor(project[rows, h, cols], w["W"][rows, :], w["eye"][rows, rows],
                                        ALU.add).then_inc(done, 1)
            dve.wait_ge(done, 5)
            nc.vector.tensor_scalar(project[re, 1, im], project[re, 0, re], -1.0, None, ALU.mult).then_inc(done, 1)


def two_fourier_layers(nc, x, conv, skip_kernel, skip_bias, fw1, fw2, W, bias, y, tables):
    B = x.shape[0]
    scratch = {}
    for name, shape, dt in (("modes_x", (B, C, K1, 2, K1), F32), ("planes", (B, 2, 2, K1, ROWS, C), F16),
                            ("mixed", (2, B, 2, K1 // 8 + 1, K1, 8, 2 * C), F32)):
        scratch[name] = nc.dram_tensor(name, shape, dt, kind="Internal").ap()
    with Memory(nc) as m:
        w = {name: m.sb(f"c_{name}", list(t.shape), t.dtype) for name, t in tables.items()}
        loads = [(w[name][:], tables[name]) for name in tables]
        for name, shape in (("skip", [P, C]), ("W", [P, C]), ("project", [P, 2, 2 * C]), ("skip_bias", [C, 1]),
                            ("bias", [1, C]), ("bias_n", [1, C])):
            w[name] = m.sb(f"w_{name}", shape)
        for d in range(2):
            loads.append((w["skip"][d * C:(d + 1) * C, :], skip_kernel))
            loads.append((w["W"][d * C:(d + 1) * C, :], W))
        loads.append((w["skip_bias"][:, :], skip_bias.unsqueeze(1)))
        loads.append((w["bias"][:, :], bias.unsqueeze(0)))
        w["conv"] = conv
        load_constants(nc, loads)
        prepare(nc, w)
        gram = m.sb("gram", [P, B, C])
        pass_1(nc, B, x, scratch["modes_x"], gram, w["rows_dft"], w["cols_dft"])
        apply = m.sb("apply", [P, B, 2, P], F16)
        with Memory(nc) as mm:
            x1_modes = mm.sb("x1_modes", [P, B, K1, 2, K1])
            fw_first = mm.sb("fw_first", [P, C, KC, 2 * K1])
            norm_0(nc, B, gram, apply, scratch["modes_x"], scratch["planes"], x1_modes, (fw1, fw2), fw_first, w)
            mixing_1(nc, B, x1_modes, (fw1, fw2), fw_first, scratch["mixed"])
        project_1(nc, B, scratch["mixed"], scratch["planes"], w)
        pass_2(nc, B, x, y, apply, scratch["planes"], w)


def kernel(x, L0_conv_conv, L0_conv_skip_kernel, L0_conv_skip_bias, L1_conv_fw1, L1_conv_fw2, L1_conv_W, L1_conv_b):
    import concourse.bacc as bacc
    from concourse.bass_utils import run_bass_kernel_spmd

    nc = bacc.Bacc("TRN2", target_bir_lowering=False, num_devices=1)
    given = {"x": x, "conv": L0_conv_conv, "skip_kernel": L0_conv_skip_kernel, "skip_bias": L0_conv_skip_bias,
             "fw1": L1_conv_fw1, "fw2": L1_conv_fw2, "W": L1_conv_W, "b": L1_conv_b}
    arrays = {}

    def take(name, a, kind="ExternalInput"):
        a = np.ascontiguousarray(a)
        arrays[name] = a
        return nc.dram_tensor(name, a.shape, mybir.dt.from_np(a.dtype), kind=kind).ap()

    args = [take(f"in_{name}", a) for name, a in given.items()]
    tables = {name: take(f"table_{name}", a) for name, a in dft_constants().items()}
    y = nc.dram_tensor("out_y", np.shape(x), F32, kind="ExternalOutput").ap()
    two_fourier_layers(nc, *args, y, tables)
    return run_bass_kernel_spmd(nc, [arrays], core_ids=[0]).results[0]["out_y"]
```
